# Optimizing a Trainium2 kernel written in Bass

```python
import numpy as np
import jax
import jax.numpy as jnp

def _softmax(x, axis=-1):
    return jax.nn.softmax(x, axis=axis)

def _gelu(x):
    return jax.nn.gelu(x, approximate=True)

def _silu(x):
    return jax.nn.silu(x)

def _sigmoid(x):
    return jax.nn.sigmoid(x)

def _layernorm(x, axis=-1, eps=1e-05):
    m = jnp.mean(x, axis=axis, keepdims=True)
    v = jnp.var(x, axis=axis, keepdims=True)
    return (x - m) / jnp.sqrt(v + eps)

def _scatter_add(tgt, idx, src, axis=0):
    return tgt.at[idx].add(src)

def _segment_sum(src, seg, n):
    return jax.ops.segment_sum(src, seg, n)
kernel_name = 'mk_conv_seq_d2_conv_nhwc768_r4_f8eabc'

def setup_inputs(seed: int=0):
    np.random.seed(seed)
    _w = jnp.asarray

    def _rec_inputs():
        import jax
        import jax.numpy as jnp
        _gk = jax.random.key(seed)
        x = -0.0002221 + 1 * jax.random.normal(jax.random.fold_in(_gk, 1), (8, 16, 16, 192), jnp.float32)
        return x
    x = _rec_inputs()

    def _L0_conv_setup():
        import jax, jax.numpy as jnp
        import numpy as np
        B, H, W, D = (8, 16, 16, 192)
        HEADS, WS = (12, 14)
        HD = D // HEADS
        MLP = 4 * D
        LREL = 2 * WS - 1
        EPS = 1e-05

        def _layer_norm(x, w, b):
            mu = jnp.mean(x, axis=-1, keepdims=True)
            var = jnp.mean(jnp.square(x - mu), axis=-1, keepdims=True)
            return (x - mu) * jax.lax.rsqrt(var + EPS) * w + b
        key = jax.random.key(seed)
        ks = jax.random.split(key, 12)
        s = 0.02
        return {'x': jax.random.normal(ks[0], (B, H, W, D), jnp.float32), 'qkv_w': jax.random.normal(ks[1], (D, 3 * D), jnp.float32) * s, 'qkv_b': jax.random.normal(ks[2], (3 * D,), jnp.float32) * s, 'proj_w': jax.random.normal(ks[3], (D, D), jnp.float32) * s, 'proj_b': jax.random.normal(ks[4], (D,), jnp.float32) * s, 'rel_pos_h': jax.random.normal(ks[5], (LREL, HD), jnp.float32) * s, 'rel_pos_w': jax.random.normal(ks[6], (LREL, HD), jnp.float32) * s, 'norm1_w': jnp.ones((D,), jnp.float32), 'norm1_b': jnp.zeros((D,), jnp.float32), 'norm2_w': jnp.ones((D,), jnp.float32), 'norm2_b': jnp.zeros((D,), jnp.float32), 'fc1_w': jax.random.normal(ks[7], (D, MLP), jnp.float32) * s, 'fc1_b': jax.random.normal(ks[8], (MLP,), jnp.float32) * s, 'fc2_w': jax.random.normal(ks[9], (MLP, D), jnp.float32) * s, 'fc2_b': jax.random.normal(ks[10], (D,), jnp.float32) * s}
    _L0_conv_all = _L0_conv_setup()
    _L0_conv_in = {k: v for k, v in _L0_conv_all.items() if k in ('qkv_w', 'qkv_b', 'proj_w', 'proj_b', 'rel_pos_h', 'rel_pos_w', 'norm1_w', 'norm1_b', 'norm2_w', 'norm2_b', 'fc1_w', 'fc1_b', 'fc2_w', 'fc2_b')}
    del _L0_conv_all

    def _L1_conv_setup():
        import jax, jax.numpy as jnp
        import numpy as np
        WS = 14
        NH = 12
        HD = 16
        EPS = 1e-06
        _REL_IDX = np.arange(WS)[:, None] - np.arange(WS)[None, :] + (WS - 1)

        def _layer_norm(x, g, b):
            m = jnp.mean(x, axis=-1, keepdims=True)
            v = jnp.mean(jnp.square(x - m), axis=-1, keepdims=True)
            return (x - m) * jax.lax.rsqrt(v + EPS) * g + b
        key = jax.random.key(seed)
        ks = jax.random.split(key, 8)
        B, H, W, C = (4, 16, 16, 192)
        s = lambda fan: 1.0 / np.sqrt(fan)
        return {'x': jax.random.normal(ks[0], (B, H, W, C), jnp.float32), 'ln1_g': jnp.ones((C,), jnp.float32), 'ln1_b': jnp.zeros((C,), jnp.float32), 'w_qkv': jax.random.normal(ks[1], (C, 3 * C), jnp.float32) * s(C), 'b_qkv': jnp.zeros((3 * C,), jnp.float32), 'w_proj': jax.random.normal(ks[2], (C, C), jnp.float32) * s(C), 'b_proj': jnp.zeros((C,), jnp.float32), 'rel_pos_h': jax.random.normal(ks[3], (2 * WS - 1, HD), jnp.float32) * 0.02, 'rel_pos_w': jax.random.normal(ks[4], (2 * WS - 1, HD), jnp.float32) * 0.02, 'ln2_g': jnp.ones((C,), jnp.float32), 'ln2_b': jnp.zeros((C,), jnp.float32), 'w_fc1': jax.random.normal(ks[5], (C, 4 * C), jnp.float32) * s(C), 'b_fc1': jnp.zeros((4 * C,), jnp.float32), 'w_fc2': jax.random.normal(ks[6], (4 * C, C), jnp.float32) * s(4 * C), 'b_fc2': jnp.zeros((C,), jnp.float32)}
    _L1_conv_all = _L1_conv_setup()
    _L1_conv_in = {k: v for k, v in _L1_conv_all.items() if k in ('ln1_g', 'ln1_b', 'w_qkv', 'b_qkv', 'w_proj', 'b_proj', 'rel_pos_h', 'rel_pos_w', 'ln2_g', 'ln2_b', 'w_fc1', 'b_fc1', 'w_fc2', 'b_fc2')}
    del _L1_conv_all
    return {'x': x, 'L0_conv_qkv_w': _L0_conv_in['qkv_w'], 'L0_conv_qkv_b': _L0_conv_in['qkv_b'], 'L0_conv_proj_w': _L0_conv_in['proj_w'], 'L0_conv_proj_b': _L0_conv_in['proj_b'], 'L0_conv_rel_pos_h': _L0_conv_in['rel_pos_h'], 'L0_conv_rel_pos_w': _L0_conv_in['rel_pos_w'], 'L0_conv_norm1_w': _L0_conv_in['norm1_w'], 'L0_conv_norm1_b': _L0_conv_in['norm1_b'], 'L0_conv_norm2_w': _L0_conv_in['norm2_w'], 'L0_conv_norm2_b': _L0_conv_in['norm2_b'], 'L0_conv_fc1_w': _L0_conv_in['fc1_w'], 'L0_conv_fc1_b': _L0_conv_in['fc1_b'], 'L0_conv_fc2_w': _L0_conv_in['fc2_w'], 'L0_conv_fc2_b': _L0_conv_in['fc2_b'], 'L1_conv_ln1_g': _L1_conv_in['ln1_g'], 'L1_conv_ln1_b': _L1_conv_in['ln1_b'], 'L1_conv_w_qkv': _L1_conv_in['w_qkv'], 'L1_conv_b_qkv': _L1_conv_in['b_qkv'], 'L1_conv_w_proj': _L1_conv_in['w_proj'], 'L1_conv_b_proj': _L1_conv_in['b_proj'], 'L1_conv_rel_pos_h': _L1_conv_in['rel_pos_h'], 'L1_conv_rel_pos_w': _L1_conv_in['rel_pos_w'], 'L1_conv_ln2_g': _L1_conv_in['ln2_g'], 'L1_conv_ln2_b': _L1_conv_in['ln2_b'], 'L1_conv_w_fc1': _L1_conv_in['w_fc1'], 'L1_conv_b_fc1': _L1_conv_in['b_fc1'], 'L1_conv_w_fc2': _L1_conv_in['w_fc2'], 'L1_conv_b_fc2': _L1_conv_in['b_fc2']}

def reference(x, L0_conv_qkv_w, L0_conv_qkv_b, L0_conv_proj_w, L0_conv_proj_b, L0_conv_rel_pos_h, L0_conv_rel_pos_w, L0_conv_norm1_w, L0_conv_norm1_b, L0_conv_norm2_w, L0_conv_norm2_b, L0_conv_fc1_w, L0_conv_fc1_b, L0_conv_fc2_w, L0_conv_fc2_b, L1_conv_ln1_g, L1_conv_ln1_b, L1_conv_w_qkv, L1_conv_b_qkv, L1_conv_w_proj, L1_conv_b_proj, L1_conv_rel_pos_h, L1_conv_rel_pos_w, L1_conv_ln2_g, L1_conv_ln2_b, L1_conv_w_fc1, L1_conv_b_fc1, L1_conv_w_fc2, L1_conv_b_fc2):
    import jax
    import jax.numpy as jnp

    def _L0_conv_ref(x, qkv_w, qkv_b, proj_w, proj_b, rel_pos_h, rel_pos_w, norm1_w, norm1_b, norm2_w, norm2_b, fc1_w, fc1_b, fc2_w, fc2_b):
        import jax, jax.numpy as jnp
        import numpy as np
        B, H, W, D = (8, 16, 16, 192)
        HEADS, WS = (12, 14)
        HD = D // HEADS
        MLP = 4 * D
        LREL = 2 * WS - 1
        EPS = 1e-05

        def _layer_norm(x, w, b):
            mu = jnp.mean(x, axis=-1, keepdims=True)
            var = jnp.mean(jnp.square(x - mu), axis=-1, keepdims=True)
            return (x - mu) * jax.lax.rsqrt(var + EPS) * w + b
        shortcut = x
        xn = _layer_norm(x, norm1_w, norm1_b)
        pad_h = (WS - H % WS) % WS
        pad_w = (WS - W % WS) % WS
        Hp, Wp = (H + pad_h, W + pad_w)
        xp = jnp.pad(xn, ((0, 0), (0, pad_h), (0, pad_w), (0, 0)))
        win = xp.reshape(B, Hp // WS, WS, Wp // WS, WS, D)
        win = win.transpose(0, 1, 3, 2, 4, 5).reshape(-1, WS, WS, D)
        Bn = win.shape[0]
        N = WS * WS
        qkv = win.reshape(Bn, N, D) @ qkv_w + qkv_b
        qkv = qkv.reshape(Bn, N, 3, HEADS, HD).transpose(2, 0, 3, 1, 4)
        qkv = qkv.reshape(3, Bn * HEADS, N, HD)
        q, k, v = (qkv[0], qkv[1], qkv[2])
        scale = HD ** (-0.5)
        attn = jnp.einsum('bqc,bkc->bqk', q * scale, k)
        coords = jnp.arange(WS)[:, None] - jnp.arange(WS)[None, :] + (WS - 1)
        Rh = rel_pos_h[coords]
        Rw = rel_pos_w[coords]
        r_q = q.reshape(-1, WS, WS, HD)
        rel_h = jnp.einsum('bhwc,hkc->bhwk', r_q, Rh)
        rel_w = jnp.einsum('bhwc,wkc->bhwk', r_q, Rw)
        attn = (attn.reshape(-1, WS, WS, WS, WS) + rel_h[:, :, :, :, None] + rel_w[:, :, :, None, :]).reshape(-1, N, N)
        attn = jax.nn.softmax(attn, axis=-1)
        out = jnp.einsum('bqk,bkc->bqc', attn, v)
        out = out.reshape(Bn, HEADS, WS, WS, HD).transpose(0, 2, 3, 1, 4).reshape(Bn, WS, WS, D)
        out = out @ proj_w + proj_b
        out = out.reshape(B, Hp // WS, Wp // WS, WS, WS, D)
        out = out.transpose(0, 1, 3, 2, 4, 5).reshape(B, Hp, Wp, D)[:, :H, :W, :]
        x = shortcut + out
        xn2 = _layer_norm(x, norm2_w, norm2_b)
        h = jax.nn.gelu(xn2 @ fc1_w + fc1_b, approximate=False)
        x = x + (h @ fc2_w + fc2_b)
        return x

    def _L1_conv_ref(x, ln1_g, ln1_b, w_qkv, b_qkv, w_proj, b_proj, rel_pos_h, rel_pos_w, ln2_g, ln2_b, w_fc1, b_fc1, w_fc2, b_fc2):
        import jax, jax.numpy as jnp
        import numpy as np
        WS = 14
        NH = 12
        HD = 16
        EPS = 1e-06
        _REL_IDX = np.arange(WS)[:, None] - np.arange(WS)[None, :] + (WS - 1)

        def _layer_norm(x, g, b):
            m = jnp.mean(x, axis=-1, keepdims=True)
            v = jnp.mean(jnp.square(x - m), axis=-1, keepdims=True)
            return (x - m) * jax.lax.rsqrt(v + EPS) * g + b
        B, H, W, C = x.shape
        shortcut = x
        x = _layer_norm(x, ln1_g, ln1_b)
        pad_h = (WS - H % WS) % WS
        pad_w = (WS - W % WS) % WS
        xp = jnp.pad(x, ((0, 0), (0, pad_h), (0, pad_w), (0, 0)))
        Hp, Wp = (H + pad_h, W + pad_w)
        nH, nW = (Hp // WS, Wp // WS)
        win = xp.reshape(B, nH, WS, nW, WS, C).transpose(0, 1, 3, 2, 4, 5)
        win = win.reshape(B * nH * nW, WS * WS, C)
        Bw = win.shape[0]
        qkv = win @ w_qkv + b_qkv
        qkv = qkv.reshape(Bw, WS * WS, 3, NH, HD)
        qkv = qkv.transpose(2, 0, 3, 1, 4).reshape(3, Bw * NH, WS * WS, HD)
        q, k, v = (qkv[0], qkv[1], qkv[2])
        scale = HD ** (-0.5)
        attn = jnp.einsum('bqd,bkd->bqk', q * scale, k)
        Rh = rel_pos_h[_REL_IDX]
        Rw = rel_pos_w[_REL_IDX]
        rq = q.reshape(-1, WS, WS, HD)
        rel_h = jnp.einsum('bhwc,hkc->bhwk', rq, Rh)
        rel_w = jnp.einsum('bhwc,wkc->bhwk', rq, Rw)
        attn = attn.reshape(-1, WS, WS, WS, WS)
        attn = attn + rel_h[..., None] + rel_w[:, :, :, None, :]
        attn = attn.reshape(-1, WS * WS, WS * WS)
        attn = jax.nn.softmax(attn, axis=-1)
        out = attn @ v
        out = out.reshape(Bw, NH, WS, WS, HD).transpose(0, 2, 3, 1, 4).reshape(Bw, WS, WS, C)
        out = out @ w_proj + b_proj
        xr = out.reshape(B, nH, nW, WS, WS, C).transpose(0, 1, 3, 2, 4, 5)
        xr = xr.reshape(B, Hp, Wp, C)[:, :H, :W, :]
        x = shortcut + xr
        y = _layer_norm(x, ln2_g, ln2_b)
        y = jax.nn.gelu(y @ w_fc1 + b_fc1, approximate=False)
        y = y @ w_fc2 + b_fc2
        return x + y

    def _gn(v, G=32, eps=1e-05):
        B_, H_, W_, C_ = v.shape
        g = v.reshape(B_, H_, W_, G, C_ // G)
        m = jnp.mean(g, axis=(1, 2, 4), keepdims=True)
        s = jnp.var(g, axis=(1, 2, 4), keepdims=True)
        return ((g - m) / jnp.sqrt(s + eps)).reshape(v.shape)

    def _ln_c(v, eps=1e-06):
        m = jnp.mean(v, axis=-1, keepdims=True)
        s = jnp.var(v, axis=-1, keepdims=True)
        return (v - m) / jnp.sqrt(s + eps)

    def _ln_t(v, eps=1e-05):
        m = jnp.mean(v, axis=-1, keepdims=True)
        s = jnp.var(v, axis=-1, keepdims=True)
        return (v - m) / jnp.sqrt(s + eps)

    def _to_tokens(v):
        B_, H_, W_, C_ = v.shape
        return v.reshape(B_, H_ * W_, C_)

    def _from_tokens(t, like):
        return t.reshape(like.shape)
    x = _L0_conv_ref(x, L0_conv_qkv_w, L0_conv_qkv_b, L0_conv_proj_w, L0_conv_proj_b, L0_conv_rel_pos_h, L0_conv_rel_pos_w, L0_conv_norm1_w, L0_conv_norm1_b, L0_conv_norm2_w, L0_conv_norm2_b, L0_conv_fc1_w, L0_conv_fc1_b, L0_conv_fc2_w, L0_conv_fc2_b)
    x = _L1_conv_ref(x, L1_conv_ln1_g, L1_conv_ln1_b, L1_conv_w_qkv, L1_conv_b_qkv, L1_conv_w_proj, L1_conv_b_proj, L1_conv_rel_pos_h, L1_conv_rel_pos_w, L1_conv_ln2_g, L1_conv_ln2_b, L1_conv_w_fc1, L1_conv_b_fc1, L1_conv_w_fc2, L1_conv_b_fc2)
    return x

_drawn_inputs = setup_inputs


def setup_inputs(seed=0):
    import zlib

    import numpy as np

    out = dict(_drawn_inputs(seed))
    spreads = {'L0_conv_norm1_w': (1.0, 0.6),
     'L0_conv_norm1_b': (0.0, 0.684),
     'L0_conv_norm2_w': (1.0, 0.6),
     'L0_conv_norm2_b': (0.0, 0.771),
     'L1_conv_ln1_g': (1.0, 0.2),
     'L1_conv_ln1_b': (0.0, 0.1),
     'L1_conv_b_qkv': (0.0, 0.1),
     'L1_conv_b_proj': (0.0, 0.1),
     'L1_conv_ln2_g': (1.0, 0.2),
     'L1_conv_ln2_b': (0.0, 0.1),
     'L1_conv_b_fc1': (0.0, 0.1),
     'L1_conv_b_fc2': (0.0, 0.1)}
    factors = {'L0_conv_qkv_w': 4.289,
     'L0_conv_qkv_b': 7.315,
     'L0_conv_proj_w': 3.749,
     'L0_conv_rel_pos_h': 8.0,
     'L0_conv_rel_pos_w': 8.0,
     'L0_conv_fc1_b': 7.739,
     'L1_conv_rel_pos_h': 6.089,
     'L1_conv_rel_pos_w': 5.899,
     'L0_conv_proj_b': 4.606,
     'L0_conv_fc2_b': 4.467}
    for name, (base, spread) in spreads.items():
        noise = np.random.default_rng([zlib.crc32(name.encode()), seed]).standard_normal(out[name].shape)
        drawn = base * np.exp(spread * noise) if base else spread * noise
        out[name] = jnp.asarray(drawn.astype(out[name].dtype))
    for name, factor in factors.items():
        out[name] = (out[name] * factor).astype(out[name].dtype)
    return out
```

```python
from contextlib import ExitStack

import concourse.bass as bass
from concourse import mybir

F32 = mybir.dt.float32
F32R = mybir.dt.float32r
ALU = mybir.AluOpType
ACT = mybir.ActivationFunctionType
AX = mybir.AxisListType.X

P = 128
IMAGES, SIDE, D = 8, 16, 192
TOK = SIDE * SIDE
TILES = TOK // P
HEADS = 12
HD = D // HEADS
WS = 14
EDGE = SIDE - WS
MLP = 4 * D
MC = MLP // P
LO = D - P
QKV = 3 * D
WCOLS = 2 * D + 2 * P
GH = HEADS // 2
GF = GH * HD
GR = GH * WS
VW = HD + 1
NSEG = 3
NEG = -1.0e30
SETUP_POOL = TILES + 2
SETUP_DVE = 2 * (2 + 2)
COLS = 4 + 4 + MC + 2
W_LOADS = 16 * 2 * (3 + 2 + 3)
EPS = (1e-5, 1e-6)

R_QLO, R_RHI, R_RLO, R_MASK, R_MAX = 2 * HD, 3 * HD, 3 * HD + 2 * WS, 3 * HD + 4 * WS, 3 * HD + 4 * WS + 4
KROWS = 3 * HD

LAYER_IN = ["qkv_w", "qkv_b", "proj_w", "proj_b", "fc1_w", "fc2_w", "fc2_b"]
CONSTS = ["ident", "key_rows", "query_mask", "pad_mask", "head_mask"]


def build(nc, x, layers, const, out):
    x_t = x.rearrange("b h w d -> (b h w) d").rearrange("(t p) d -> p t d", p=P)
    out_t = out.rearrange("b h w d -> (b h w) d").rearrange("(t p) d -> p t d", p=P)

    with ExitStack() as ctx:
        def sb(name, shape, dt=F32):
            return ctx.enter_context(nc.sbuf_tensor(name, shape, dt))

        def sem(name):
            return ctx.enter_context(nc.semaphore(name))

        X = sb("X", [P, IMAGES * TILES, D])
        ident = sb("ident", [P, P])
        key_rows = sb("key_rows", [P, TOK])
        query_mask = sb("query_mask", [P, TILES, 4])
        pad_mask = sb("pad_mask", [P, NSEG, TILES * HEADS])
        head_mask = sb("head_mask", [GF, GH])
        minus_half = sb("minus_half", [P, TILES])
        wqkv_in = sb("wqkv_in", [P, 2, WCOLS])
        w1_in = sb("w1_in", [P, 2, MLP])
        wqkv_hi, wqkv_lo = sb("wqkv_hi", [P, 2, WCOLS], F32R), sb("wqkv_lo", [P, 2, WCOLS], F32R)
        w1_hi, w1_lo = sb("w1_hi", [P, 2, MLP], F32R), sb("w1_lo", [P, 2, MLP], F32R)
        wp, w2, qkvb, pb, b2, columns, n1, n2, b1, rel, rel_blocks, kb, kb_blocks = ([] for _ in range(13))
        for L in range(2):
            wp.append(sb(f"wp{L}", [P, 2, D]))
            w2.append(sb(f"w2{L}", [P, MC, D]))
            qkvb.append(sb(f"qkvb{L}", [P, QKV]))
            pb.append(sb(f"pb{L}", [P, D]))
            b2.append(sb(f"b2{L}", [P, D]))
            columns.append(sb(f"columns{L}", [P, COLS]))
            n1.append(columns[L][:, 0:4].rearrange("p (c w) -> p c w", c=2))
            n2.append(columns[L][:, 4:8].rearrange("p (c w) -> p c w", c=2))
            b1.append(columns[L][:, 8:8 + MC])
            rel.append(sb(f"rel{L}", [GF, 2, 2 * WS - 1]))
            rel_blocks.append(sb(f"rel_blocks{L}", [GF, 2 * WS, GH, WS]))
            kb.append(columns[L][0:GF, 8 + MC:COLS])
            kb_blocks.append(sb(f"kb_blocks{L}", [GF, 2, GH]))
        norm_s = [sb(f"norm_s{i}", [P, TILES, 6]) for i in range(2)]
        norm_mv = [sb(f"norm_mv{i}", [P, TILES, 2]) for i in range(2)]
        norm_var = [sb(f"norm_var{i}", [P, TILES]) for i in range(2)]
        norm_rstd = [sb(f"norm_rstd{i}", [P, TILES]) for i in range(2)]
        xhat = [sb(f"xhat{i}", [P, TILES, 2 * P]) for i in range(2)]
        xn = [sb(f"xn{i}", [P, 2, TOK]) for i in range(2)]
        xn_hi = [sb(f"xn_hi{i}", [P, 2, TOK], F32R) for i in range(2)]
        xn_lo = [sb(f"xn_lo{i}", [P, TOK], F32R) for i in range(2)]
        qk = sb("qk", [P, TILES, 2 * D])
        q_t = sb("q_t", [GF, 2, TOK])
        rel_t = sb("rel_t", [GR, 2, 2, TOK])
        RW = 2 * HEADS * WS + HEADS
        rel_tok = sb("rel_tok", [P, TILES, RW])
        q_stack_tok = sb("q_stack_tok", [P, TILES, HEADS, P], F32R)
        k_stack_tok = sb("k_stack_tok", [P, TILES, HEADS, KROWS], F32R)
        q_stack = [sb(f"q_stack{i}", [P, HEADS, TOK], F32R) for i in range(2)]
        k_stack = [sb(f"k_stack{i}", [P, HEADS, TOK], F32R) for i in range(2)]
        v_ones = [sb(f"v_ones{i}", [P, TILES, HEADS, VW]) for i in range(2)]
        pad_e = sb("pad_e", [P, TILES * 2 * HEADS, WS])
        seg_max = [sb(f"seg_max{i}", [P, TILES, 2, HEADS]) for i in range(2)]
        seg_sum = [sb(f"seg_sum{i}", [P, TILES, 2, HEADS]) for i in range(2)]
        pad_max = sb("pad_max", [P, NSEG, TILES, HEADS])
        pad_prod = sb("pad_prod", [P, NSEG, TILES, HEADS])
        pad_top = sb("pad_top", [P, TILES * HEADS])
        pad_w = sb("pad_w", [P, NSEG, TILES * HEADS])
        row_max = sb("row_max", [P, HEADS, TILES])
        top = sb("top", [P, TILES, HEADS])
        neg_top = sb("neg_top", [P, TILES, 2, HEADS], F32R)
        neg_top_t = sb("neg_top_t", [2 * HEADS, TOK], F32R)
        pad_sum = [sb(f"pad_sum{i}", [P, TILES, HEADS]) for i in range(2)]
        pad_out = [sb(f"pad_out{i}", [P, TILES, HEADS, HD]) for i in range(2)]
        NP = 3
        probs = [sb(f"probs{i}", [P, 2, TOK]) for i in range(NP)]
        den = sb("den", [P, TILES, HEADS])
        att = sb("att", [P, TILES, D])
        att_t = sb("att_t", [P, 2, TOK])
        hid = sb("hid", [P, MC, TOK])

        XB = [ctx.enter_context(nc.psum_tensor(f"xb{i}", [P, 512], F32)) for i in range(3)]
        YB = [ctx.enter_context(nc.psum_tensor(f"yb{i}", [P, 512], F32)) for i in range(5)]

        s_x0, s_x, s_const = sem("x0_loaded"), sem("x_loaded"), sem("const_loaded")
        s_w, s_wx, s_wy = sem("weights_loaded"), sem("wqkv_loaded"), sem("w1_loaded")
        s_zero = sem("buffers_zeroed")
        s_setup = sem("setup_done")
        s_kb = sem("k_bias_scaled")
        s_wxs, s_wxh, s_wxl = sem("wqkv_scaled"), sem("wqkv_hi_done"), sem("wqkv_lo_done")
        s_wyh, s_wyl = sem("w1_hi_done"), sem("w1_lo_done")
        n_stat = [sem(f"norm{i}_stats") for i in range(2)]
        n_aggr = [sem(f"norm{i}_aggregated") for i in range(2)]
        n_var = [sem(f"norm{i}_var") for i in range(2)]
        n_rstd = [sem(f"norm{i}_rstd") for i in range(2)]
        n_hat = [sem(f"norm{i}_hat") for i in range(2)]
        n_tr = [sem(f"norm{i}_transposed") for i in range(2)]
        n_aff = [sem(f"norm{i}_affine") for i in range(2)]
        n_hi = [sem(f"norm{i}_hi") for i in range(2)]
        n_lo = [sem(f"norm{i}_lo") for i in range(2)]
        s_qkv, s_qkvo = sem("qkv_product"), sem("qkv_biased")
        s_qt, s_qto = sem("q_transposed"), sem("q_t_ready")
        s_qkh, s_qkl = sem("qk_hi"), sem("qk_lo")
        s_rel, s_relo = sem("rel_product"), sem("rel_t_ready")
        s_rt, s_rto = sem("rel_transposed"), sem("rel_tok_ready")
        s_rhi, s_rlo = sem("rel_hi"), sem("rel_lo")
        s_pmax, s_psub, s_pexp = sem("pad_segment_max"), sem("pad_shifted"), sem("pad_exp")
        s_psum, s_pcomb, s_pmask, s_pqb, s_ptop = (sem(n) for n in (
            "pad_segment_sum", "pad_combined", "pad_masked", "pad_with_q_bias", "pad_top"))
        s_sq, s_sk = sem("q_stack_transposed"), sem("k_stack_transposed")
        s_sqo, s_sko = sem("q_stack_ready"), sem("k_stack_ready")
        s_s, s_smax = sem("scores_by_query"), sem("row_max")
        s_top, s_nhi, s_nlo = sem("top"), sem("neg_top_hi"), sem("neg_top_lo")
        s_nt, s_nto, s_nd = sem("neg_top_transposed"), sem("neg_top_t_ready"), sem("neg_top_stacked")
        s_wsub, s_wexp, s_wmul, s_padsum, s_padout = (sem(n) for n in (
            "pad_weight_arg", "pad_weight_exp", "pad_weight", "pad_sum", "pad_out"))
        s_st, s_ex, s_av = sem("scores_by_key"), sem("probs"), sem("prob_times_v")
        s_n1, s_n2, s_att = sem("att_sums"), sem("att_reciprocal"), sem("att_normalised")
        s_at, s_ato, s_pr = sem("att_transposed"), sem("att_t_ready"), sem("projection")
        s_xb, s_xa, s_xb2 = sem("x_plus_proj_bias"), sem("x_after_attention"), sem("x_plus_fc2_bias")
        s_f1, s_ge, s_f2, s_xm = sem("fc1"), sem("gelu"), sem("fc2"), sem("x_after_mlp")
        s_out = sem("out_stored")

        def settle(eng, n):
            if not isinstance(n, int):
                eng.nop(nofuse=True)

        def x_slot(n0, n):
            return X[:, bass.ds((n - n0) * TILES, TILES), :] if not isinstance(n, int) \
                else X[:, (n - n0) * TILES:(n - n0 + 1) * TILES, :]

        def run(eng, part_a, part_b, at_layer):
            at_layer(0)
            part_a(None, (0, 0, 0))
            part_b(None, (0, 0, 0))
            for L in range(2):
                base = IMAGES * L

                def step(n, y_par):
                    y = (n, L, y_par)
                    xi = (n + 1, L, 1 - y_par)
                    part_a(y, xi)
                    part_b(y, xi)

                step(base, 0)
                with eng.Fori(0, IMAGES // 2 - 1, 1) as j:
                    step(base + j * 2 + 1, 1)
                    step(base + j * 2 + 2, 0)
                y = (base + IMAGES - 1, L, 1)
                if L == 0:
                    at_layer(1)
                    part_a(y, (base + IMAGES, 1, 0))
                    part_b(y, (base + IMAGES, 1, 0))
                else:
                    part_a(y, None)
                    part_b(y, None)

        def base_of(L):
            return IMAGES * L

        block = ctx.enter_context(nc.Block())

        @block.sync
        def _(sp):
            def load_wqkv(L):
                w = layers[L]["qkv_w"]
                sp.dma_start(wqkv_in[:, 0, 0:QKV], w[0:P, :]).then_inc(s_wx, 16)
                sp.dma_start(wqkv_in[0:LO, 1, 0:QKV], w[P:D, :]).then_inc(s_wx, 16)
                sp.dma_start(wqkv_in[LO:P, 1, 0:QKV], w[P:D, :]).then_inc(s_wx, 16)

            def load_w1(L):
                w = layers[L]["fc1_w"]
                sp.dma_start(w1_in[:, 0, :], w[0:P, :]).then_inc(s_wy, 16)
                sp.dma_start(w1_in[0:LO, 1, :], w[P:D, :]).then_inc(s_wy, 16)
                sp.dma_start(w1_in[LO:P, 1, :], w[P:D, :]).then_inc(s_wy, 16)

            sp.dma_start(x_slot(0, 0), x_t[:, 0:TILES, :]).then_inc(s_x0, 16)
            load_wqkv(0)
            for name, tile in zip(CONSTS, (ident, key_rows, query_mask, pad_mask, head_mask)):
                sp.dma_start(tile[:], const[name]).then_inc(s_const, 16)
            for L in range(2):
                p = layers[L]
                for tile, name in ((qkvb[L], "qkv_b"), (pb[L], "proj_b"), (b2[L], "fc2_b")):
                    sp.dma_start(tile[:, :], p[name].unsqueeze(0).broadcast_to([P, tile.shape[1]])).then_inc(s_w, 16)
                sp.dma_start(rel[L][:, :, :], p["rel"]).then_inc(s_w, 16)
                sp.dma_start(columns[L][:, :], p["columns"]).then_inc(s_w, 16)
                sp.dma_start(wp[L][:, 0, :], p["proj_w"][0:P, :]).then_inc(s_w, 16)
                sp.dma_start(wp[L][0:LO, 1, :], p["proj_w"][P:D, :]).then_inc(s_w, 16)
                sp.dma_start(w2[L][:, :, :], p["fc2_w"].rearrange("(m f) n -> f m n", f=P)).then_inc(s_w, 16)
                if L == 0:
                    load_w1(0)
                    sp.dma_start(X[:, TILES:, :], x_t[:, TILES:, :]).then_inc(s_x, 16)
            sp.wait_ge(s_wxl, 1)
            sp.wait_ge(s_wxh, 1)
            load_wqkv(1)
            sp.wait_ge(s_wyl, 1)
            sp.wait_ge(s_wyh, 1)
            load_w1(1)

            def stack_neg_top(xi):
                n, L, par = xi
                sp.wait_ge(s_nto, n + 1)
                settle(sp, n)
                sp.wait_ge(s_s, HEADS * (n + 1))
                settle(sp, n)
                for part in range(2):
                    sp.dma_start(q_stack[par][R_MAX + part:R_MAX + part + 1, :, :].bitcast(F32),
                                 neg_top_t[part * HEADS:(part + 1) * HEADS, :].bitcast(F32)).then_inc(s_nd, 16)

            def part_a(y, xi):
                if y is not None and y[1] == 1 and not isinstance(y[0], int):
                    pass

            def part_b(y, xi):
                if xi is not None:
                    stack_neg_top(xi)
                if y is not None and y[1] == 1:
                    n = y[0]
                    sp.wait_ge(s_xm, n + 1)
                    settle(sp, n)
                    slot = x_slot(IMAGES, n)
                    dst = out_t[:, bass.ds((n - IMAGES) * TILES, TILES), :] if not isinstance(n, int) \
                        else out_t[:, (n - IMAGES) * TILES:(n - IMAGES + 1) * TILES, :]
                    sp.dma_start(dst, slot).then_inc(s_out, 16)

            run(sp, part_a, part_b, lambda L: None)
            sp.wait_ge(s_out, 16 * IMAGES)

        @block.gpsimd
        def _(pool):
            pool.memset(wqkv_in[:, :, QKV:WCOLS], 0.0).then_inc(s_zero, 1)
            pool.memset(minus_half[:, :], -0.5).then_inc(s_zero, 1)
            for par in range(2):
                pool.memset(v_ones[par][:, :, :, HD:VW], 1.0).then_inc(s_zero, 1)
            pool.memset(q_stack_tok[:, :, :, :].bitcast(F32), 0.0).then_inc(s_zero, 1)
            pool.wait_ge(s_zero, 5)
            pool.wait_ge(s_const, 16 * len(CONSTS))
            for a in range(TILES):
                pool.tensor_copy(q_stack_tok[:, a, :, R_MASK:R_MASK + 4],
                                 query_mask[:, a, :].unsqueeze(1).broadcast_to([P, HEADS, 4])).then_inc(s_setup, 1)
            for par in range(2):
                pool.tensor_copy(k_stack[par][:, :, :],
                                 key_rows[:, :].unsqueeze(1).broadcast_to([P, HEADS, TOK])).then_inc(s_setup, 1)

            def rstd(i, n):
                pool.wait_ge(n_var[i], n + 1)
                pool.wait_ge(n_hat[i], n)
                pool.tensor_tensor(norm_rstd[i][:, :], norm_var[i][:, :], minus_half[:, :],
                                   ALU.pow).then_inc(n_rstd[i], 1)

            def split_hi(i, n):
                pool.wait_ge(n_aff[i], n + 1)
                if i == 0:
                    pool.wait_ge(s_qkv, TILES * n)
                else:
                    pool.wait_ge(s_f1, MC * n)
                pool.wait_ge(n_lo[i], n)
                settle(pool, n)
                pool.tensor_copy(xn_hi[i][:, :, :], xn[i][:, :, :]).then_inc(n_hi[i], 1)

            def part_a(y, xi):
                if y is not None:
                    n, L, par = y
                    pool.wait_ge(n_hat[0], n + 1)
                    pool.wait_ge(s_w, W_LOADS)
                    settle(pool, n)
                    xs = x_slot(base_of(L), n)
                    pool.tensor_tensor(xs, xs, pb[L][:, :].unsqueeze(1).broadcast_to([P, TILES, D]),
                                       ALU.add).then_inc(s_xb, 1)
                if xi is not None:
                    n, L, par = xi
                    rstd(0, n)
                    split_hi(0, n)
                    pool.wait_ge(s_qkvo, TILES * (n + 1))
                    pool.wait_ge(s_sq, GH * n)
                    pool.wait_ge(s_sk, GH * n)
                    pool.wait_ge(s_qkl, n)
                    settle(pool, n)
                    for a in range(TILES):
                        q_in = qk[:, a, 0:D].rearrange("p (h c) -> p h c", c=HD)
                        k_in = qk[:, a, D:2 * D].rearrange("p (h c) -> p h c", c=HD)
                        pool.tensor_copy(
                            q_stack_tok[:, a, :, 0:2 * HD].rearrange("p h (t c) -> p h t c", t=2),
                            q_in.unsqueeze(2).broadcast_to([P, HEADS, 2, HD]))
                        last = pool.tensor_copy(k_stack_tok[:, a, :, 0:HD], k_in)
                        last = pool.tensor_copy(k_stack_tok[:, a, :, 2 * HD:3 * HD], k_in)
                    last.then_inc(s_qkh, 1)
                    pool.wait_ge(s_rto, TILES * (n + 1))
                    settle(pool, n)
                    for a in range(TILES):
                        for w in range(2):
                            last = pool.tensor_copy(
                                q_stack_tok[:, a, :, R_RHI + w * WS:R_RHI + (w + 1) * WS],
                                rel_tok[:, a, w * HEADS * WS:(w + 1) * HEADS * WS].rearrange("p (h k) -> p h k", k=WS))
                    last.then_inc(s_rhi, 1)
                    pool.wait_ge(s_pmax, n + 1)
                    pool.wait_ge(s_psum, n)
                    for a in range(TILES):
                        src = rel_tok[:, a, 0:2 * HEADS * WS].rearrange("p (h k) -> p h k", k=WS)
                        dst = pad_e[:, a * 2 * HEADS:(a + 1) * 2 * HEADS, :]
                        for s, (lo, hi) in enumerate(((0, EDGE), (EDGE, WS))):
                            m = seg_max[s][:, a, :, :].rearrange("p w h -> p (w h)").unsqueeze(2)
                            last = pool.tensor_tensor(dst[:, :, lo:hi], src[:, :, lo:hi],
                                                      m.broadcast_to([P, 2 * HEADS, hi - lo]), ALU.subtract)
                    last.then_inc(s_psub, 1)

            def part_b(y, xi):
                if y is not None:
                    n, L, par = y
                    rstd(1, n)
                    split_hi(1, n)
                    pool.wait_ge(n_hat[1], n + 1)
                    settle(pool, n)
                    xs = x_slot(base_of(L), n)
                    pool.tensor_tensor(xs, xs, b2[L][:, :].unsqueeze(1).broadcast_to([P, TILES, D]),
                                       ALU.add).then_inc(s_xb2, 1)
                if xi is not None:
                    n, L, par = xi
                    pool.wait_ge(s_padsum, n + 1)
                    if not (isinstance(n, int) and n < 2):
                        pool.wait_ge(s_att, n - 1)
                    for a in range(TILES):
                        last = pool.tensor_tensor(
                            pad_out[par][:, a, :, :],
                            qkvb[L][:, 2 * D:QKV].rearrange("p (h c) -> p h c", c=HD),
                            pad_sum[par][:, a, :].unsqueeze(2).broadcast_to([P, HEADS, HD]), ALU.mult)
                    last.then_inc(s_padout, 1)

            run(pool, part_a, part_b, lambda L: None)

        @block.scalar
        def _(act):
            def at_layer(L):
                act.wait_ge(s_wxs, L + 1)
                if L:
                    act.wait_ge(s_qkv, TILES * IMAGES * L)
                act.activation(wqkv_hi[:, :, :], wqkv_in[:, :, :], ACT.Copy).then_inc(s_wxh, 1)
                if L == 0:
                    split_w1(0)

            def split_w1(L):
                act.wait_ge(s_wy, 48 * (L + 1))
                if L:
                    act.wait_ge(s_f1, MC * IMAGES * L)
                act.activation(w1_hi[:, :, :], w1_in[:, :, :], ACT.Copy).then_inc(s_wyh, 1)

            def affine(i, n, L, bank):
                act.wait_ge(n_tr[i], n + 1)
                act.wait_ge(n_hi[i], n)
                act.wait_ge(n_lo[i], n)
                act.wait_ge(s_w, W_LOADS)
                norm = (n1, n2)[i][L]
                for c in range(2):
                    last = act.activation(xn[i][:, c, :], bank[:, c * TOK:(c + 1) * TOK], ACT.Identity,
                                          bias=norm[:, c, 1:2], scale=norm[:, c, 0:1])
                last.then_inc(n_aff[i], 1)

            def exps(y, h):
                n, L, par = y
                act.wait_ge(s_st, HEADS * n + h + 1)
                if h >= NP:
                    act.wait_ge(s_av, HEADS * n + h - NP + 1)
                else:
                    act.wait_ge(s_av, HEADS * n)
                act.activation(probs[h % NP][:, :, :], YB[h % 2][:, :].rearrange("p (k t) -> p k t", k=2),
                               ACT.Exp).then_inc(s_ex, 1)

            def x_front(k, xi):
                n, L, par = xi
                if k == 1:
                    affine(0, n, L, XB[0])
                if k == 6:
                    act.wait_ge(s_qt, n + 1)
                    act.wait_ge(s_rel, n)
                    act.wait_ge(s_rt, TILES * n)
                    act.activation(q_t[:, :, :], XB[2][0:GF, :].rearrange("p (g t) -> p g t", g=2),
                                   ACT.Copy).then_inc(s_qto, 1)
                if k == 8:
                    act.wait_ge(s_rel, n + 1)
                    act.wait_ge(s_rt, TILES * n)
                    act.activation(rel_t[:, 0, :, :], XB[0][0:GR, :].rearrange("p (g t) -> p g t", g=2), ACT.Copy)
                    for g in range(2):
                        last = act.activation(
                            rel_t[:, 1, g, :].rearrange("p (r c) -> p r c", c=SIDE),
                            XB[1][0:GR, g * TOK:(g + 1) * TOK].rearrange("p (c r) -> p r c", r=SIDE), ACT.Copy)
                    last.then_inc(s_relo, 1)
                if k == 10:
                    act.wait_ge(s_ptop, n)
                    act.wait_ge(s_rlo, n)
                    act.wait_ge(s_psub, n)
                    for a in range(TILES):
                        act.wait_ge(s_rt, TILES * n + a + 1)
                        act.activation(rel_tok[:, a, :], (XB[2], XB[0])[a][:, 0:RW], ACT.Copy).then_inc(s_rto, 1)
                if k == 12:
                    act.wait_ge(s_psub, n + 1)
                    act.activation(pad_e[:, :, :], pad_e[:, :, :], ACT.Exp).then_inc(s_pexp, 1)

            def part_a(y, xi):
                for k in range(HEADS + 1):
                    if y is not None and k < HEADS:
                        exps(y, k)
                    if xi is not None:
                        x_front(k, xi)
                if y is not None and isinstance(y[0], int) and y[0] == IMAGES:
                    split_w1(1)

            def stack_out(xi, hp):
                n, L, par = xi
                act.wait_ge(s_sq, GH * n + hp + 1)
                if not (isinstance(n, int) and n < 2):
                    act.wait_ge(s_st, HEADS * (n - 1))
                act.activation(q_stack[par][:, 2 * hp:2 * hp + 2, :],
                               XB[0][:, :].rearrange("p (h t) -> p h t", h=2), ACT.Copy).then_inc(s_sqo, 1)
                act.wait_ge(s_sk, GH * n + hp + 1)
                act.wait_ge(s_setup, SETUP_POOL + SETUP_DVE)
                act.activation(k_stack[par][0:KROWS, 2 * hp:2 * hp + 2, :],
                               XB[1][0:KROWS, :].rearrange("p (h t) -> p h t", h=2), ACT.Copy).then_inc(s_sko, 1)

            def gelus(y, m):
                n, L, par = y
                act.wait_ge(s_f1, MC * n + 2 * (m // 2) + 2)
                act.wait_ge(s_f2, TILES * n)
                act.activation(hid[:, m, :], YB[(4, 0, 1)[m // 2]][:, (m % 2) * TOK:(m % 2 + 1) * TOK], ACT.Gelu,
                               bias=b1[L][:, m:m + 1]).then_inc(s_ge, 1)

            def y_back(h, y):
                n, L, par = y
                if h == 1:
                    act.wait_ge(s_at, n + 1)
                    act.wait_ge(s_pr, n)
                    act.activation(att_t[:, 0, :], YB[3][:, 0:TOK], ACT.Copy)
                    act.activation(att_t[0:LO, 1, :], YB[3][0:LO, TOK:2 * TOK], ACT.Copy).then_inc(s_ato, 1)
                if h == 4:
                    affine(1, n, L, YB[3])
                if h in (7, 8, 9):
                    gelus(y, 2 * (h - 7))
                    gelus(y, 2 * (h - 7) + 1)

            def part_b(y, xi):
                if xi is not None:
                    stack_out(xi, 0)
                for h in range(HEADS):
                    if xi is not None and h % 2 == 0 and h // 2 + 1 < GH:
                        stack_out(xi, h // 2 + 1)
                    if y is not None:
                        y_back(h, y)
                if xi is not None:
                    n, L, par = xi
                    act.wait_ge(s_nt, n + 1)
                    act.wait_ge(s_nd, 32 * n)
                    act.activation(neg_top_t[:, :], XB[2][0:2 * HEADS, 0:TOK], ACT.Copy).then_inc(s_nto, 1)
                    act.wait_ge(s_wsub, n + 1)
                    act.activation(pad_w[:, :, :], pad_w[:, :, :], ACT.Exp).then_inc(s_wexp, 1)

            run(act, part_a, part_b, at_layer)

        @block.vector
        def _(dve):
            def at_layer(L):
                dve.wait_ge(s_wx, 48 * (L + 1))
                dve.wait_ge(s_zero, 5)
                dve.tensor_scalar(wqkv_in[:, :, D:2 * D], wqkv_in[:, :, D:2 * D], HD ** -0.5, None,
                                  ALU.mult).then_inc(s_wxs, 1)
                dve.wait_ge(s_wxs, L + 1)
                dve.wait_ge(s_wxh, L + 1)
                dve.tensor_tensor(wqkv_lo[:, :, :], wqkv_in[:, :, :], wqkv_hi[:, :, :].bitcast(F32),
                                  ALU.subtract).then_inc(s_wxl, 1)
                if L == 0:
                    dve.wait_ge(s_w, W_LOADS)
                    dve.wait_ge(s_const, 16 * len(CONSTS))
                    for l in range(2):
                        dve.tensor_scalar(qkvb[l][:, D:2 * D], qkvb[l][:, D:2 * D], HD ** -0.5, None,
                                          ALU.mult).then_inc(s_setup, 1)
                        dve.tensor_scalar(kb[l], kb[l], HD ** -0.5, None, ALU.mult).then_inc(s_kb, 1)
                        dve.wait_ge(s_kb, l + 1)
                        dve.tensor_tensor(kb_blocks[l][:, :, :],
                                          head_mask[:, :].unsqueeze(1).broadcast_to([GF, 2, GH]),
                                          kb[l].unsqueeze(2).broadcast_to([GF, 2, GH]),
                                          ALU.mult).then_inc(s_setup, 1)
                        for w in range(2):
                            src = rel[l][:, w, 0:WS]
                            slide = bass.AP(src.tensor, src.offset, [list(src.ap[0]), [1, WS], [0, GH], [1, WS]])
                            dve.tensor_tensor(
                                rel_blocks[l][:, w * WS:(w + 1) * WS, :, :], slide,
                                head_mask[:, :].unsqueeze(1).unsqueeze(3).broadcast_to([GF, WS, GH, WS]),
                                ALU.mult).then_inc(s_setup, 1)
                    split_w1(0)

            def split_w1(L):
                dve.wait_ge(s_wyh, L + 1)
                dve.wait_ge(s_wy, 48 * (L + 1))
                dve.tensor_tensor(w1_lo[:, :, :], w1_in[:, :, :], w1_hi[:, :, :].bitcast(F32),
                                  ALU.subtract).then_inc(s_wyl, 1)

            def norm(i, n, L):
                xs = x_slot(base_of(L), n)
                dve.wait_ge(n_aggr[i], n)
                settle(dve, n)
                for a in range(TILES):
                    last = dve.bn_stats(norm_s[i][:, a, :], xs[:, a, :])
                last.then_inc(n_stat[i], 1)
                dve.wait_ge(n_stat[i], n + 1)
                dve.wait_ge(n_hat[i], n)
                settle(dve, n)
                for a in range(TILES):
                    last = dve.bn_aggr(norm_mv[i][:, a, :], norm_s[i][:, a, :])
                last.then_inc(n_aggr[i], 1)
                dve.wait_ge(n_aggr[i], n + 1)
                dve.wait_ge(n_rstd[i], n)
                dve.tensor_scalar(norm_var[i][:, :], norm_mv[i][:, :, 1], EPS[L], None, ALU.add).then_inc(n_var[i], 1)
                dve.wait_ge(n_rstd[i], n + 1)
                dve.wait_ge(n_tr[i], n)
                for a in range(TILES):
                    mean, r = norm_mv[i][:, a, 0:1], norm_rstd[i][:, a:a + 1]
                    dve.tensor_scalar(xhat[i][:, a, 0:P], xs[:, a, 0:P], mean, r, ALU.subtract, ALU.mult)
                    last = dve.tensor_scalar(
                        xhat[i][:, a, P:2 * P].rearrange("p (t f) -> p t f", t=2),
                        xs[:, a, P:D].unsqueeze(1).broadcast_to([P, 2, LO]), mean, r, ALU.subtract, ALU.mult)
                last.then_inc(n_hat[i], 1)

            def split_lo(i, n):
                dve.wait_ge(n_hi[i], n + 1)
                dve.wait_ge(n_aff[i], n + 1)
                dve.wait_ge(s_qkv if i == 0 else s_f1, (TILES if i == 0 else MC) * n)
                dve.tensor_tensor(xn_lo[i][:, :], xn[i][:, 0, :], xn_hi[i][:, 0, :].bitcast(F32), ALU.subtract)
                dve.tensor_tensor(xn_hi[i][LO:P, 1, :], xn[i][LO:P, 1, :], xn_hi[i][LO:P, 1, :].bitcast(F32),
                                  ALU.subtract).then_inc(n_lo[i], 1)

            def x_front(k, xi):
                n, L, par = xi
                if k == 0:
                    if isinstance(n, int) and n == 0:
                        dve.wait_ge(s_x0, 16)
                    else:
                        dve.wait_ge(s_x, 16)
                    if L == 1:
                        dve.wait_ge(s_xm, n - IMAGES + 1)
                    norm(0, n, L)
                if k == 2:
                    split_lo(0, n)
                if k in (4, 5):
                    a = k - 4
                    dve.wait_ge(s_qkv, TILES * n + a + 1)
                    dve.wait_ge(s_setup, SETUP_POOL + SETUP_DVE)
                    if a == 0:
                        dve.wait_ge(s_qkh, n)
                        dve.wait_ge(s_qkl, n)
                        dve.wait_ge(s_qt, n)
                        if not (isinstance(n, int) and n < 2):
                            dve.wait_ge(s_av, HEADS * (n - 1))
                    dve.tensor_tensor(qk[:, a, :], (XB[1], XB[0])[a][:, 0:2 * D], qkvb[L][:, 0:2 * D], ALU.add)
                    dve.tensor_tensor(v_ones[par][:, a, :, 0:HD],
                                      (XB[2], XB[1])[a][:, 0:D].rearrange("p (h c) -> p h c", c=HD),
                                      qkvb[L][:, 2 * D:QKV].rearrange("p (h c) -> p h c", c=HD),
                                      ALU.add).then_inc(s_qkvo, 1)
                if k == 7:
                    dve.wait_ge(s_qkh, n + 1)
                    dve.wait_ge(s_sq, GH * n)
                    dve.wait_ge(s_sk, GH * n)
                    dve.tensor_tensor(
                        q_stack_tok[:, :, :, R_QLO:R_QLO + HD],
                        qk[:, :, 0:D].rearrange("p a (h c) -> p a h c", c=HD),
                        q_stack_tok[:, :, :, 0:HD].bitcast(F32), ALU.subtract)
                    dve.tensor_tensor(
                        k_stack_tok[:, :, :, HD:2 * HD],
                        qk[:, :, D:2 * D].rearrange("p a (h c) -> p a h c", c=HD),
                        k_stack_tok[:, :, :, 0:HD].bitcast(F32), ALU.subtract).then_inc(s_qkl, 1)
                if k == 11:
                    dve.wait_ge(s_rto, TILES * (n + 1))
                    dve.wait_ge(s_psub, n)
                    dve.wait_ge(s_pcomb, n)
                    rows = rel_tok[:, :, 0:2 * HEADS * WS].rearrange("p a (h k) -> p a h k", k=WS)
                    for s, (lo, hi) in enumerate(((0, EDGE), (EDGE, WS))):
                        last = dve.tensor_reduce(seg_max[s][:, :, :, :].rearrange("p a w h -> p a (w h)"),
                                                 rows[:, :, :, lo:hi], AX, ALU.max)
                    last.then_inc(s_pmax, 1)
                    dve.wait_ge(s_rhi, n + 1)
                    for a in range(TILES):
                        last = dve.tensor_tensor(
                            q_stack_tok[:, a, :, R_RLO:R_RLO + 2 * WS].rearrange("p h (w k) -> p w h k", w=2),
                            rel_tok[:, a, 0:2 * HEADS * WS].rearrange("p (w h k) -> p w h k", w=2, k=WS),
                            q_stack_tok[:, a, :, R_RHI:R_RHI + 2 * WS].rearrange("p h (w k) -> p w h k", w=2).bitcast(F32),
                            ALU.subtract)
                    last.then_inc(s_rlo, 1)
                if k == 12:
                    dve.wait_ge(s_pexp, n + 1)
                    dve.wait_ge(s_pcomb, n)
                    for s, (lo, hi) in enumerate(((0, EDGE), (EDGE, WS))):
                        last = dve.tensor_reduce(
                            seg_sum[s][:, :, :, :].rearrange("p a w h -> p (a w h)"), pad_e[:, :, lo:hi], AX, ALU.add)
                    last.then_inc(s_psum, 1)
                    dve.wait_ge(s_psum, n + 1)
                    dve.wait_ge(s_wsub, n)
                    dve.wait_ge(s_wmul, n)
                    dve.wait_ge(s_ptop, n)
                    for seg, (hs, ws) in enumerate(((0, 1), (1, 1), (1, 0))):
                        dve.tensor_tensor(pad_max[:, seg, :, :], seg_max[hs][:, :, 0, :], seg_max[ws][:, :, 1, :], ALU.add)
                        last = dve.tensor_tensor(pad_prod[:, seg, :, :], seg_sum[hs][:, :, 0, :],
                                                 seg_sum[ws][:, :, 1, :], ALU.mult)
                    last.then_inc(s_pcomb, 1)
                    dve.wait_ge(s_pcomb, n + 1)
                    flat = pad_max[:, :, :, :].rearrange("p s a h -> p s (a h)")
                    dve.tensor_tensor(flat, flat, pad_mask[:, :, :], ALU.add).then_inc(s_pmask, 1)
                    dve.wait_ge(s_pmask, n + 1)
                    dve.tensor_tensor(pad_max[:, :, :, :], pad_max[:, :, :, :],
                                      rel_tok[:, :, 2 * HEADS * WS:RW].unsqueeze(1).broadcast_to(
                                          [P, NSEG, TILES, HEADS]), ALU.add).then_inc(s_pqb, 1)
                    dve.wait_ge(s_pqb, n + 1)
                    dve.wait_ge(s_top, n)
                    dve.tensor_reduce(pad_top[:, :], pad_max[:, :, :, :].rearrange("p s a h -> p (a h) s"), AX,
                                      ALU.max).then_inc(s_ptop, 1)

            def part_a(y, xi):
                for k in range(HEADS + 1):
                    if xi is not None:
                        x_front(k, xi)
                if y is not None and isinstance(y[0], int) and y[0] == IMAGES:
                    split_w1(1)

            def row_maxima(xi, h):
                n, L, par = xi
                dve.wait_ge(s_s, HEADS * n + h + 1)
                if h == 0:
                    dve.wait_ge(s_top, n)
                dve.tensor_reduce(row_max[:, h, :], XB[2][:, :].rearrange("p (a t) -> p a t", a=TILES), AX,
                                  ALU.max).then_inc(s_smax, 1)

            def y_back(h, y):
                n, L, par = y
                if h == 0:
                    dve.wait_ge(s_av, HEADS * (n + 1))
                    dve.wait_ge(s_padout, n + 1)
                    dve.wait_ge(s_at, n)
                    dve.wait_ge(s_att, n)
                    o = YB[2][:, :].rearrange("p (a t) -> p a t", a=TILES)[:, :, 0:HEADS * VW] \
                        .rearrange("p a (h c) -> p a h c", c=VW)
                    a4 = att[:, :, :].rearrange("p a (h c) -> p a h c", c=HD)
                    dve.tensor_tensor(a4, o[:, :, :, 0:HD], pad_out[par][:, :, :, :], ALU.add)
                    dve.tensor_tensor(den[:, :, :], o[:, :, :, HD], pad_sum[par][:, :, :], ALU.add).then_inc(s_n1, 1)
                    dve.wait_ge(s_n1, n + 1)
                    dve.reciprocal(den[:, :, :], den[:, :, :]).then_inc(s_n2, 1)
                    dve.wait_ge(s_n2, n + 1)
                    dve.tensor_tensor(a4, a4, den[:, :, :].unsqueeze(3).broadcast_to([P, TILES, HEADS, HD]),
                                      ALU.mult).then_inc(s_att, 1)
                xs = x_slot(base_of(L), n)
                if h == 2:
                    dve.wait_ge(s_pr, n + 1)
                    dve.wait_ge(s_xb, n + 1)
                    dve.tensor_tensor(xs, xs, YB[4][:, 0:TILES * D].rearrange("p (a d) -> p a d", d=D),
                                      ALU.add).then_inc(s_xa, 1)
                if h == 3:
                    dve.wait_ge(s_xa, n + 1)
                    norm(1, n, L)
                if h == 5:
                    split_lo(1, n)
                if h == 11:
                    dve.wait_ge(s_f2, TILES * (n + 1))
                    dve.wait_ge(s_xb2, n + 1)
                    dve.tensor_tensor(xs, xs, YB[2][:, 0:TILES * D].rearrange("p (a d) -> p a d", d=D),
                                      ALU.add).then_inc(s_xm, 1)

            def part_b(y, xi):
                for h in range(HEADS):
                    if y is not None:
                        y_back(h, y)
                    if xi is not None:
                        row_maxima(xi, h)
                if xi is not None:
                    n, L, par = xi
                    dve.wait_ge(s_smax, HEADS * (n + 1))
                    dve.wait_ge(s_ptop, n + 1)
                    dve.wait_ge(s_nlo, n)
                    dve.wait_ge(s_wsub, n)
                    dve.tensor_tensor(top[:, :, :], row_max[:, :, :].rearrange("p h a -> p a h"),
                                      pad_top[:, :].rearrange("p (a h) -> p a h", a=TILES), ALU.max).then_inc(s_top, 1)
                    dve.wait_ge(s_top, n + 1)
                    dve.wait_ge(s_nt, n)
                    dve.tensor_scalar(neg_top[:, :, 0, :], top[:, :, :], -1.0, None, ALU.mult).then_inc(s_nhi, 1)
                    dve.wait_ge(s_nhi, n + 1)
                    dve.scalar_tensor_tensor(neg_top[:, :, 1, :], top[:, :, :], -1.0, neg_top[:, :, 0, :].bitcast(F32),
                                             ALU.mult, ALU.subtract).then_inc(s_nlo, 1)
                    dve.wait_ge(s_padsum, n)
                    dve.tensor_tensor(pad_w[:, :, :], pad_max[:, :, :, :].rearrange("p s a h -> p s (a h)"),
                                      top[:, :, :].rearrange("p a h -> p (a h)").unsqueeze(1).broadcast_to(
                                          [P, NSEG, TILES * HEADS]), ALU.subtract).then_inc(s_wsub, 1)
                    dve.wait_ge(s_wexp, n + 1)
                    dve.tensor_tensor(pad_w[:, :, :], pad_w[:, :, :],
                                      pad_prod[:, :, :, :].rearrange("p s a h -> p s (a h)"),
                                      ALU.mult).then_inc(s_wmul, 1)
                    dve.wait_ge(s_wmul, n + 1)
                    if not (isinstance(n, int) and n < 2):
                        dve.wait_ge(s_att, n - 1)
                        dve.wait_ge(s_padout, n - 1)
                    dve.tensor_reduce(pad_sum[par][:, :, :].rearrange("p a h -> p (a h)"),
                                      pad_w[:, :, :].rearrange("p s k -> p k s"), AX, ALU.add).then_inc(s_padsum, 1)

            run(dve, part_a, part_b, at_layer)

        @block.tensor
        def _(pe):
            def split_product(psum, chunks):
                for i, (lhs, rhs) in enumerate(chunks):
                    last = pe.matmul(psum, lhs, rhs, start=(i == 0), stop=(i == len(chunks) - 1))
                return last

            def norm_transposes(i, n, bank):
                pe.wait_ge(n_hat[i], n + 1)
                for c in range(2):
                    for a in range(TILES):
                        last = pe.transpose(bank[:, c * TOK + a * P:c * TOK + (a + 1) * P],
                                            xhat[i][:, a, c * P:(c + 1) * P], ident[:, :])
                last.then_inc(n_tr[i], 1)

            def x_front(k, xi):
                n, L, par = xi
                if k == 0:
                    pe.wait_ge(s_sqo, GH * n)
                    pe.wait_ge(s_const, 16 * len(CONSTS))
                    norm_transposes(0, n, XB[0])
                if k in (3, 4):
                    a = k - 3
                    if a == 0:
                        pe.wait_ge(n_lo[0], n + 1)
                        pe.wait_ge(s_wxl, L + 1)
                        pe.wait_ge(s_sko, GH * n)
                        pe.wait_ge(s_nto, n)
                    else:
                        pe.wait_ge(n_aff[0], n + 1)
                        pe.wait_ge(s_qkvo, TILES * n + 1)
                    tok = slice(a * P, (a + 1) * P)
                    for bank, cols in (((XB[1], XB[0])[a], slice(0, 2 * D)), ((XB[2], XB[1])[a], slice(2 * D, WCOLS))):
                        last = split_product(bank[:, 0:cols.stop - cols.start], [
                            (xn_hi[0][:, 0, tok], wqkv_hi[:, 0, cols]), (xn_hi[0][:, 0, tok], wqkv_lo[:, 0, cols]),
                            (xn_lo[0][:, tok], wqkv_hi[:, 0, cols]),
                            (xn_hi[0][:, 1, tok], wqkv_hi[:, 1, cols]), (xn_hi[0][:, 1, tok], wqkv_lo[:, 1, cols])])
                    last.then_inc(s_qkv, 1)
                if k == 6:
                    pe.wait_ge(s_qkvo, TILES * (n + 1))
                    for g in range(2):
                        for a in range(TILES):
                            last = pe.transpose(XB[2][0:GF, g * TOK + a * P:g * TOK + (a + 1) * P],
                                                qk[:, a, g * GF:(g + 1) * GF], ident[:, :])
                    last.then_inc(s_qt, 1)
                if k == 7:
                    pe.wait_ge(s_qto, n + 1)
                    pe.wait_ge(s_setup, SETUP_POOL + SETUP_DVE)
                    for w in range(2):
                        grid = q_t[:, :, :].rearrange("p g (r c) -> p g r c" if w == 0 else "p g (r c) -> p g c r", c=SIDE)
                        dst = XB[w][0:GR, :].rearrange("p (g r c) -> p g r c", g=2, c=SIDE)
                        for i in range(WS):
                            at = slice(i, i + WS + 1, WS) if i < EDGE else slice(i, i + 1)
                            last = pe.matmul(dst[:, :, at, :], rel_blocks[L][:, w * WS + WS - 1 - i, :, :]
                                             .rearrange("p h k -> p (h k)"), grid[:, :, at, :], start=True, stop=True)
                    last.then_inc(s_rel, 1)
                if k == 9:
                    pe.wait_ge(s_relo, n + 1)
                    for a in range(TILES):
                        bank = (XB[2], XB[0])[a]
                        for w in range(2):
                            for g in range(2):
                                col = (w * 2 + g) * GR
                                pe.transpose(bank[:, col:col + GR], rel_t[:, w, g, a * P:(a + 1) * P],
                                             ident[0:GR, 0:GR])
                        for g in range(2):
                            col = 4 * GR + g * GH
                            last = pe.matmul(bank[:, col:col + GH], q_t[:, g, a * P:(a + 1) * P],
                                             kb_blocks[L][:, g, :], start=True, stop=True)
                        last.then_inc(s_rt, 1)

            def scores_by_key(y, h):
                n, L, par = y
                if h == 0:
                    pe.wait_ge(s_nd, 32 * (n + 1))
                    pe.wait_ge(s_ge, MC * n)
                if h >= 2:
                    pe.wait_ge(s_ex, HEADS * n + h - 1)
                for c in range(2):
                    last = pe.matmul(YB[h % 2][:, c * TOK:(c + 1) * TOK], k_stack[par][:, h, c * P:(c + 1) * P],
                                     q_stack[par][:, h, :], start=True, stop=True)
                last.then_inc(s_st, 1)

            def times_v(y, h):
                n, L, par = y
                if h == 0:
                    pe.wait_ge(s_xm, n)
                pe.wait_ge(s_ex, HEADS * n + h + 1)
                for a in range(TILES):
                    for c in range(2):
                        last = pe.matmul(YB[2][:, a * TOK + h * VW:a * TOK + (h + 1) * VW],
                                         probs[h % NP][:, c, a * P:(a + 1) * P], v_ones[par][:, c, h, :],
                                         start=(c == 0), stop=(c == 1))
                last.then_inc(s_av, 1)

            def part_a(y, xi):
                for k in range(HEADS + 1):
                    if y is not None:
                        if k < HEADS:
                            scores_by_key(y, k)
                        if k > 0:
                            times_v(y, k - 1)
                    if xi is not None:
                        x_front(k, xi)

            def stack_transposes(xi, hp):
                n, L, par = xi
                if hp == 0:
                    pe.wait_ge(s_rto, TILES * (n + 1))
                    pe.wait_ge(s_relo, n + 1)
                    pe.wait_ge(s_qkl, n + 1)
                    pe.wait_ge(s_rlo, n + 1)
                    pe.wait_ge(s_rhi, n + 1)
                else:
                    pe.wait_ge(s_sqo, GH * n + hp)
                for h in range(2):
                    for a in range(TILES):
                        last = pe.transpose(XB[0][:, h * TOK + a * P:h * TOK + (a + 1) * P],
                                            q_stack_tok[:, a, 2 * hp + h, :].bitcast(F32), ident[:, :])
                last.then_inc(s_sq, 1)
                if hp:
                    pe.wait_ge(s_sko, GH * n + hp)
                    settle(pe, n)
                for h in range(2):
                    for a in range(TILES):
                        last = pe.transpose(XB[1][0:KROWS, h * TOK + a * P:h * TOK + (a + 1) * P],
                                            k_stack_tok[:, a, 2 * hp + h, :].bitcast(F32), ident[:, :])
                last.then_inc(s_sk, 1)

            def scores_by_query(xi, h):
                n, L, par = xi
                if h % 2 == 0:
                    pe.wait_ge(s_sqo, GH * n + h // 2 + 1)
                    pe.wait_ge(s_sko, GH * n + h // 2 + 1)
                if h == 0:
                    pe.wait_ge(s_rto, TILES * (n + 1))
                else:
                    pe.wait_ge(s_smax, HEADS * n + h)
                for a in range(TILES):
                    last = pe.matmul(XB[2][:, a * TOK:(a + 1) * TOK], q_stack[par][:, h, a * P:(a + 1) * P],
                                     k_stack[par][:, h, :], start=True, stop=True)
                last.then_inc(s_s, 1)

            def fc1(y, m):
                n, L, par = y
                if m == 0:
                    pe.wait_ge(n_lo[1], n + 1)
                    pe.wait_ge(s_wyl, L + 1)
                    pe.wait_ge(s_xa, n + 1)
                    pe.wait_ge(s_ex, HEADS * (n + 1))
                f = slice(m * P, (m + 1) * P)
                last = split_product(YB[(4, 0, 1)[m // 2]][:, (m % 2) * TOK:(m % 2 + 1) * TOK], [
                    (w1_hi[:, 0, f], xn_hi[1][:, 0, :]), (w1_lo[:, 0, f], xn_hi[1][:, 0, :]),
                    (w1_hi[:, 0, f], xn_lo[1][:, :]),
                    (w1_hi[:, 1, f], xn_hi[1][:, 1, :]), (w1_lo[:, 1, f], xn_hi[1][:, 1, :])])
                last.then_inc(s_f1, 1)

            def y_back(h, y):
                n, L, par = y
                if h == 1:
                    pe.wait_ge(s_att, n + 1)
                    pe.wait_ge(n_aff[1], n)
                    for a in range(TILES):
                        pe.transpose(YB[3][:, a * P:(a + 1) * P], att[:, a, 0:P], ident[:, :])
                        last = pe.transpose(YB[3][0:LO, TOK + a * P:TOK + (a + 1) * P], att[:, a, P:D], ident[:, :])
                    last.then_inc(s_at, 1)
                if h == 2:
                    pe.wait_ge(s_ato, n + 1)
                    pe.wait_ge(s_ge, MC * n)
                    for a in range(TILES):
                        last = split_product(YB[4][:, a * D:(a + 1) * D], [
                            (att_t[:, 0, a * P:(a + 1) * P], wp[L][:, 0, :]),
                            (att_t[0:LO, 1, a * P:(a + 1) * P], wp[L][0:LO, 1, :])])
                    last.then_inc(s_pr, 1)
                if h == 4:
                    pe.wait_ge(s_ato, n + 1)
                    norm_transposes(1, n, YB[3])
                if h in (6, 7, 8):
                    fc1(y, 2 * (h - 6))
                    fc1(y, 2 * (h - 6) + 1)
                if h in (10, 11):
                    a = h - 10
                    if a == 0:
                        pe.wait_ge(s_att, n + 1)
                    for m in range(MC):
                        if a == 0:
                            pe.wait_ge(s_ge, MC * n + m + 1)
                        last = pe.matmul(YB[2][:, a * D:(a + 1) * D], hid[:, m, a * P:(a + 1) * P], w2[L][:, m, :],
                                         start=(m == 0), stop=(m == MC - 1))
                    last.then_inc(s_f2, 1)

            def part_b(y, xi):
                if xi is not None:
                    stack_transposes(xi, 0)
                for h in range(HEADS):
                    if xi is not None:
                        if h % 2 == 0 and h // 2 + 1 < GH:
                            stack_transposes(xi, h // 2 + 1)
                        scores_by_query(xi, h)
                    if y is not None:
                        y_back(h, y)
                if xi is not None:
                    n, L, par = xi
                    pe.wait_ge(s_nlo, n + 1)
                    pe.wait_ge(s_smax, HEADS * (n + 1))
                    for a in range(TILES):
                        last = pe.transpose(XB[2][0:2 * HEADS, a * P:(a + 1) * P],
                                            neg_top[:, a, :, :].rearrange("p t h -> p (t h)").bitcast(F32), ident[:, :])
                    last.then_inc(s_nt, 1)

            run(pe, part_a, part_b, lambda L: None)


def kernel(**inputs):
    import numpy as np
    import concourse.bacc as bacc
    from concourse.bass_utils import run_bass_kernel_spmd

    nc = bacc.Bacc("TRN2", target_bir_lowering=False, num_devices=1)
    arrays = {}

    def dram(name, a):
        a = np.ascontiguousarray(a)
        arrays[name] = a
        return nc.dram_tensor(name, a.shape, mybir.dt.from_np(a.dtype), kind="ExternalInput").ap()

    names = [dict(qkv_w="L0_conv_qkv_w", qkv_b="L0_conv_qkv_b", proj_w="L0_conv_proj_w", proj_b="L0_conv_proj_b",
                  rel_h="L0_conv_rel_pos_h", rel_w="L0_conv_rel_pos_w", n1_w="L0_conv_norm1_w",
                  n1_b="L0_conv_norm1_b", n2_w="L0_conv_norm2_w", n2_b="L0_conv_norm2_b", fc1_w="L0_conv_fc1_w",
                  fc1_b="L0_conv_fc1_b", fc2_w="L0_conv_fc2_w", fc2_b="L0_conv_fc2_b"),
             dict(qkv_w="L1_conv_w_qkv", qkv_b="L1_conv_b_qkv", proj_w="L1_conv_w_proj", proj_b="L1_conv_b_proj",
                  rel_h="L1_conv_rel_pos_h", rel_w="L1_conv_rel_pos_w", n1_w="L1_conv_ln1_g", n1_b="L1_conv_ln1_b",
                  n2_w="L1_conv_ln2_g", n2_b="L1_conv_ln2_b", fc1_w="L1_conv_w_fc1", fc1_b="L1_conv_b_fc1",
                  fc2_w="L1_conv_w_fc2", fc2_b="L1_conv_b_fc2")]
    x = dram("in_x", inputs["x"])
    layers = []
    for L, of in enumerate(names):
        layer = {k: dram(f"in_{k}_{L}", inputs[of[k]]) for k in LAYER_IN}
        columns = np.zeros((P, COLS), np.float32)
        for at, name in enumerate(("n1_w", "n1_b", "n2_w", "n2_b")):
            v, at = np.asarray(inputs[of[name]]), at + 2 * (at // 2)
            columns[:, at] = v[:P]
            columns[:, at + 2] = np.tile(v[P:], 2)
        columns[:, 8:8 + MC] = np.asarray(inputs[of["fc1_b"]]).reshape(MC, P).T
        columns[:GF, 8 + MC:] = np.asarray(inputs[of["qkv_b"]])[D:2 * D].reshape(2, GF).T
        layer["columns"] = dram(f"in_columns_{L}", columns)
        rels = [np.tile(np.asarray(inputs[of[r]])[::-1].T, (GH, 1)) for r in ("rel_h", "rel_w")]
        layer["rel"] = dram(f"in_rel_{L}", np.stack(rels, axis=1))
        layers.append(layer)

    r, c = np.divmod(np.arange(TOK), SIDE)
    window = 2 * (r >= WS) + (c >= WS)
    rows = np.zeros((P, TOK), np.float32)
    t = np.arange(TOK)
    for at in (R_RHI, R_RLO):
        rows[at + r % WS, t] = 1
        rows[at + WS + c % WS, t] = 1
    rows[R_MASK + window, t] = 1
    rows[R_MAX:R_MAX + 2] = 1
    w_tile = window.reshape(TILES, P).T
    q_mask = np.where(w_tile[:, :, None] == np.arange(4), 0, NEG).astype(np.float32)
    in_seg = np.stack([np.isin(w_tile, s) for s in ((1, 3), (1, 2, 3), (2, 3))], axis=1)
    p_mask = np.repeat(np.where(in_seg, 0, NEG)[:, :, :, None], HEADS, axis=3).reshape(P, NSEG, -1).astype(np.float32)
    h_mask = (np.arange(GF)[:, None] // HD == np.arange(GH)).astype(np.float32)
    const = {k: dram("c_" + k, a) for k, a in zip(CONSTS, (np.eye(P, dtype=np.float32), rows, q_mask, p_mask, h_mask))}

    out = nc.dram_tensor("out", (IMAGES, SIDE, SIDE, D), F32, kind="ExternalOutput").ap()
    build(nc, x, layers, const, out)
    r = run_bass_kernel_spmd(nc, [arrays], core_ids=[0])
    return r.results[0]["out"]
```

```python
from contextlib import ExitStack

import concourse.bass as bass
from concourse import mybir

F32 = mybir.dt.float32
F32R = mybir.dt.float32r
ALU = mybir.AluOpType
ACT = mybir.ActivationFunctionType
AX = mybir.AxisListType.X

P = 128
IMAGES, SIDE, D = 8, 16, 192
TOK = SIDE * SIDE
TILES = TOK // P
HEADS = 12
HD = D // HEADS
WS = 14
EDGE = SIDE - WS
MLP = 4 * D
MC = MLP // P
LO = D - P
QKV = 3 * D
WCOLS = 2 * D + 2 * P
GH = HEADS // 2
GF = GH * HD
GR = GH * WS
VW = HD + 1
NSEG = 3
NEG = -1.0e30
SETUP_DVE = 2 * 3
STACK_SETUP = 2 * (TILES + 1)
ZEROED = 2 + 2 + 2
COLS = 4 + 4 + MC + 2
V_LOADS = 16 * 2 * 3
W_LOADS = 16 * 2 * 5
STACK_ON_DVE = [h % 3 == 1 for h in range(HEADS)]
EPS = (1e-5, 1e-6)

R_QLO, R_RHI, R_RLO, R_MASK, R_MAX = 2 * HD, 3 * HD, 3 * HD + 2 * WS, 3 * HD + 4 * WS, 3 * HD + 4 * WS + 4
KROWS = 3 * HD

LAYER_IN = ["qkv_w", "qkv_b", "proj_w", "proj_b", "fc1_w", "fc2_w", "fc2_b"]
CONSTS = ["ident", "key_rows", "query_mask", "pad_mask", "head_mask"]


def build(nc, x, layers, const, out):
    x_t = x.rearrange("b h w d -> (b h w) d").rearrange("(t p) d -> p t d", p=P)
    out_t = out.rearrange("b h w d -> (b h w) d").rearrange("(t p) d -> p t d", p=P)

    with ExitStack() as ctx:
        def sb(name, shape, dt=F32):
            return ctx.enter_context(nc.sbuf_tensor(name, shape, dt))

        def sem(name):
            return ctx.enter_context(nc.semaphore(name))

        X = sb("X", [P, IMAGES * TILES, D])
        ident = sb("ident", [P, P])
        key_rows = sb("key_rows", [P, TOK])
        query_mask = sb("query_mask", [P, TILES, 4])
        pad_mask = sb("pad_mask", [P, NSEG, TILES * HEADS])
        head_mask = sb("head_mask", [GF, GH])
        minus_half = sb("minus_half", [P, TILES])
        wqkv_in = sb("wqkv_in", [P, 2, WCOLS])
        w1_in = sb("w1_in", [P, 2, MLP])
        wqkv_hi, wqkv_lo = sb("wqkv_hi", [P, 2, WCOLS], F32R), sb("wqkv_lo", [P, 2, WCOLS], F32R)
        w1_hi, w1_lo = sb("w1_hi", [P, 2, MLP], F32R), sb("w1_lo", [P, 2, MLP], F32R)
        wp, w2, qkvb, pb, b2, columns, n1, n2, b1, rel, rel_heads, kb, kb_blocks = ([] for _ in range(13))
        for L in range(2):
            wp.append(sb(f"wp{L}", [P, 2, D]))
            w2.append(sb(f"w2{L}", [P, MC, D]))
            qkvb.append(sb(f"qkvb{L}", [P, QKV]))
            pb.append(sb(f"pb{L}", [P, D]))
            b2.append(sb(f"b2{L}", [P, D]))
            columns.append(sb(f"columns{L}", [P, COLS]))
            n1.append(columns[L][:, 0:4].rearrange("p (c w) -> p c w", c=2))
            n2.append(columns[L][:, 4:8].rearrange("p (c w) -> p c w", c=2))
            b1.append(columns[L][:, 8:8 + MC])
            rel.append(sb(f"rel{L}", [GF, 2, 2 * WS - 1]))
            rel_heads.append(sb(f"rel_heads{L}", [GF, 2, 2 * WS - 1, GH]))
            kb.append(columns[L][0:GF, 8 + MC:COLS])
            kb_blocks.append(sb(f"kb_blocks{L}", [GF, 2, GH]))
        norm_s = [sb(f"norm_s{i}", [P, TILES, 6]) for i in range(2)]
        norm_mv = [sb(f"norm_mv{i}", [P, TILES, 2]) for i in range(2)]
        norm_var = [sb(f"norm_var{i}", [P, TILES]) for i in range(2)]
        norm_rstd = [sb(f"norm_rstd{i}", [P, TILES]) for i in range(2)]
        xhat = [sb(f"xhat{i}", [P, TILES, 2 * P]) for i in range(2)]
        xn = [sb(f"xn{i}", [P, 2, TOK]) for i in range(2)]
        xn_hi = [sb(f"xn_hi{i}", [P, 2, TOK], F32R) for i in range(2)]
        xn_lo = [sb(f"xn_lo{i}", [P, TOK], F32R) for i in range(2)]
        qk = sb("qk", [P, TILES, 2 * D])
        q_t = sb("q_t", [GF, 2, TOK])
        rel_t = sb("rel_t", [GR, 2, 2, TOK])
        RW = 2 * HEADS * WS + HEADS
        rel_tok = sb("rel_tok", [P, TILES, RW])
        q_stack_tok = [sb(f"q_stack_tok{i}", [P, TILES, HEADS, P], F32R) for i in range(2)]
        k_stack_tok = [sb(f"k_stack_tok{i}", [P, TILES, HEADS, KROWS], F32R) for i in range(2)]
        v_new = sb("v_new", [P, TILES, D])
        q_stack = [sb(f"q_stack{i}", [P, HEADS, TOK], F32R) for i in range(2)]
        k_stack = [sb(f"k_stack{i}", [P, HEADS, TOK], F32R) for i in range(2)]
        v_ones = [sb(f"v_ones{i}", [P, TILES, HEADS, VW]) for i in range(2)]
        pad_e = sb("pad_e", [P, TILES * 2 * HEADS, WS])
        seg_max = [sb(f"seg_max{i}", [P, TILES, 2, HEADS]) for i in range(2)]
        seg_sum = [sb(f"seg_sum{i}", [P, TILES, 2, HEADS]) for i in range(2)]
        pad_max = sb("pad_max", [P, NSEG, TILES, HEADS])
        pad_prod = sb("pad_prod", [P, NSEG, TILES, HEADS])
        pad_top = sb("pad_top", [P, TILES * HEADS])
        pad_w = sb("pad_w", [P, NSEG, TILES * HEADS])
        row_max = sb("row_max", [P, HEADS, TILES])
        top = sb("top", [P, TILES, HEADS])
        neg_top = sb("neg_top", [P, TILES, 2, HEADS], F32R)
        neg_top_t = sb("neg_top_t", [2 * HEADS, TOK], F32R)
        pad_sum = sb("pad_sum", [P, TILES, HEADS])
        pad_out = sb("pad_out", [P, TILES, HEADS, HD])
        NP = 2
        probs = [sb(f"probs{i}", [P, 2, TOK]) for i in range(NP)]
        den = sb("den", [P, TILES, HEADS])
        att = sb("att", [P, TILES, D])
        att_t = sb("att_t", [P, 2, TOK])
        hid = sb("hid", [P, MC, TOK])

        def bank(name):
            return ctx.enter_context(nc.psum_tensor(name, [P, 512], F32))

        FB = bank("front")
        TB, QB = bank("stack_transposes"), bank("by_query")
        KB = [bank(f"by_key{i}") for i in range(2)]
        VB = bank("times_v")
        BB = [bank(f"back{i}") for i in range(2)]

        def fc1_psum(m):
            return BB[(1, 0, 1)[m // 2]][:, (m % 2) * TOK:(m % 2 + 1) * TOK]

        s_x0, s_x, s_const = sem("x0_loaded"), sem("x_loaded"), sem("const_loaded")
        s_vec, s_w, s_wx, s_wy = sem("vectors_loaded"), sem("weights_loaded"), sem("wqkv_loaded"), sem("w1_loaded")
        s_zero = sem("buffers_zeroed")
        s_setup, s_stack0 = sem("vectors_ready"), sem("stack_constants_ready")
        s_kb = sem("k_bias_scaled")
        s_wxs, s_wxh, s_wxl = sem("wqkv_scaled"), sem("wqkv_hi_done"), sem("wqkv_lo_done")
        s_wyh, s_wyl = sem("w1_hi_done"), sem("w1_lo_done")
        n_stat = [sem(f"norm{i}_stats") for i in range(2)]
        n_aggr = [sem(f"norm{i}_aggregated") for i in range(2)]
        n_var = [sem(f"norm{i}_var") for i in range(2)]
        n_rstd = [sem(f"norm{i}_rstd") for i in range(2)]
        n_hat = [sem(f"norm{i}_hat") for i in range(2)]
        n_tr = [sem(f"norm{i}_transposed") for i in range(2)]
        n_aff = [sem(f"norm{i}_affine") for i in range(2)]
        n_hi = [sem(f"norm{i}_hi") for i in range(2)]
        n_lo = [sem(f"norm{i}_lo") for i in range(2)]
        s_qkv, s_qkvo = sem("qkv_product"), sem("qkv_biased")
        s_qt, s_qto = sem("q_transposed"), sem("q_t_ready")
        s_qkh, s_qkl = sem("qk_hi"), sem("qk_lo")
        s_rel, s_relo = sem("rel_product"), sem("rel_t_ready")
        s_rt, s_rto = sem("rel_transposed"), sem("rel_tok_ready")
        s_rhi, s_rlo = sem("rel_hi"), sem("rel_lo")
        s_v = sem("v_copied")
        s_pmax, s_psub, s_pexp = sem("pad_segment_max"), sem("pad_shifted"), sem("pad_exp")
        s_psum, s_pcomb, s_pmask, s_pqb, s_ptop = (sem(n) for n in (
            "pad_segment_sum", "pad_combined", "pad_masked", "pad_with_q_bias", "pad_top"))
        s_tr = sem("stacks_transposed")
        s_sta, s_std = sem("stacks_ready_by_act"), sem("stacks_ready_by_dve")
        s_s, s_smax = sem("scores_by_query"), sem("row_max")
        s_top, s_nhi, s_nlo = sem("top"), sem("neg_top_hi"), sem("neg_top_lo")
        s_nt, s_nto, s_nd = sem("neg_top_transposed"), sem("neg_top_t_ready"), sem("neg_top_stacked")
        s_padhalf = sem("pad_sum_of_two")
        s_wsub, s_wexp, s_wmul, s_padsum, s_padout = (sem(n) for n in (
            "pad_weight_arg", "pad_weight_exp", "pad_weight", "pad_sum", "pad_out"))
        s_st, s_ex, s_av = sem("scores_by_key"), sem("probs"), sem("prob_times_v")
        s_n1, s_n2, s_att = sem("att_sums"), sem("att_reciprocal"), sem("att_normalised")
        s_at, s_ato, s_pr = sem("att_transposed"), sem("att_t_ready"), sem("projection")
        s_xb, s_xa, s_xb2 = sem("x_plus_proj_bias"), sem("x_after_attention"), sem("x_plus_fc2_bias")
        s_f1, s_ge, s_f2, s_xm = sem("fc1"), sem("gelu"), sem("fc2"), sem("x_after_mlp")
        s_out = sem("out_stored")

        def settle(eng, n):
            if not isinstance(n, int):
                eng.nop(nofuse=True)

        def x_slot(n0, n):
            return X[:, bass.ds((n - n0) * TILES, TILES), :] if not isinstance(n, int) \
                else X[:, (n - n0) * TILES:(n - n0 + 1) * TILES, :]

        def run(eng, *steps):
            def iteration(i, items):
                for slot in range(HEADS):
                    for step in steps:
                        for d in items:
                            n, L, par = i(d)
                            step(n, L, par, slot - HEADS * d)

            def static(i):
                items = [d for d in (-2, -1, 0, 1) if 0 <= i + d < 2 * IMAGES]
                iteration(lambda d: (i + d, (i + d) // IMAGES, (i + d) % 2), items)

            for i in range(-1, 3):
                static(i)
            for L in range(2):
                first = IMAGES * L + 3
                with eng.Fori(0, (IMAGES - 4) // 2, 1) as j:
                    for odd in range(2):
                        iteration(lambda d: (j * 2 + (first + odd + d), L, (first + odd + d) % 2), (-2, -1, 0, 1))
                for i in range(first + IMAGES - 4, first + IMAGES if L == 0 else 2 * IMAGES + 2):
                    static(i)

        def peeled(n):
            return isinstance(n, int)

        def from_second(n):
            return not peeled(n) or n >= 2

        block = ctx.enter_context(nc.Block())

        @block.sync
        def _(sp):
            def load_wqkv(L):
                w = layers[L]["qkv_w"]
                sp.dma_start(wqkv_in[:, 0, 0:QKV], w[0:P, :]).then_inc(s_wx, 16)
                sp.dma_start(wqkv_in[0:LO, 1, 0:QKV], w[P:D, :]).then_inc(s_wx, 16)
                sp.dma_start(wqkv_in[LO:P, 1, 0:QKV], w[P:D, :]).then_inc(s_wx, 16)

            def load_w1(L):
                w = layers[L]["fc1_w"]
                sp.dma_start(w1_in[:, 0, :], w[0:P, :]).then_inc(s_wy, 16)
                sp.dma_start(w1_in[0:LO, 1, :], w[P:D, :]).then_inc(s_wy, 16)
                sp.dma_start(w1_in[LO:P, 1, :], w[P:D, :]).then_inc(s_wy, 16)

            sp.dma_start(x_slot(0, 0), x_t[:, 0:TILES, :]).then_inc(s_x0, 16)
            load_wqkv(0)
            for name, tile in zip(CONSTS, (ident, key_rows, query_mask, pad_mask, head_mask)):
                sp.dma_start(tile[:], const[name]).then_inc(s_const, 16)
            for L in range(2):
                p = layers[L]
                sp.dma_start(qkvb[L][:, :], p["qkv_b"].unsqueeze(0).broadcast_to([P, QKV])).then_inc(s_vec, 16)
                sp.dma_start(rel[L][:, :, :], p["rel"]).then_inc(s_vec, 16)
                sp.dma_start(columns[L][:, :], p["columns"]).then_inc(s_vec, 16)
            sp.dma_start(X[:, TILES:, :], x_t[:, TILES:, :]).then_inc(s_x, 16)
            load_w1(0)
            for L in range(2):
                p = layers[L]
                for tile, name in ((pb[L], "proj_b"), (b2[L], "fc2_b")):
                    sp.dma_start(tile[:, :], p[name].unsqueeze(0).broadcast_to([P, D])).then_inc(s_w, 16)
                sp.dma_start(wp[L][:, 0, :], p["proj_w"][0:P, :]).then_inc(s_w, 16)
                sp.dma_start(wp[L][0:LO, 1, :], p["proj_w"][P:D, :]).then_inc(s_w, 16)
                sp.dma_start(w2[L][:, :, :], p["fc2_w"].rearrange("(m f) n -> f m n", f=P)).then_inc(s_w, 16)
            sp.wait_ge(s_wxl, 1)
            sp.wait_ge(s_wxh, 1)
            load_wqkv(1)

            def stack_neg_top(n, L, par, t):
                if t == 13:
                    sp.wait_ge(s_nto, n + 1)
                    settle(sp, n)
                    sp.wait_ge(s_s, HEADS * (n + 1))
                    settle(sp, n)
                    for part in range(2):
                        sp.dma_start(q_stack[par][R_MAX + part:R_MAX + part + 1, :, :].bitcast(F32),
                                     neg_top_t[part * HEADS:(part + 1) * HEADS, :].bitcast(F32)).then_inc(s_nd, 16)

            def store(n, L, par, t):
                if t == 35 and peeled(n) and n == 0:
                    sp.wait_ge(s_wyl, 1)
                    sp.wait_ge(s_wyh, 1)
                    load_w1(1)
                if t == 35 and L == 1:
                    sp.wait_ge(s_xm, n + 1)
                    settle(sp, n)
                    dst = out_t[:, bass.ds((n - IMAGES) * TILES, TILES), :] if not peeled(n) \
                        else out_t[:, (n - IMAGES) * TILES:(n - IMAGES + 1) * TILES, :]
                    sp.dma_start(dst, x_slot(IMAGES, n)).then_inc(s_out, 16)

            run(sp, stack_neg_top, store)
            sp.wait_ge(s_out, 16 * IMAGES)

        @block.gpsimd
        def _(pool):
            pool.memset(wqkv_in[:, :, QKV:WCOLS], 0.0).then_inc(s_zero, 1)
            pool.memset(minus_half[:, :], -0.5).then_inc(s_zero, 1)
            for par in range(2):
                pool.memset(v_ones[par][:, :, :, HD:VW], 1.0).then_inc(s_zero, 1)
            pool.wait_ge(s_zero, ZEROED)
            pool.wait_ge(s_const, 16 * len(CONSTS))

            def constant_rows(par):
                for a in range(TILES):
                    pool.tensor_copy(q_stack_tok[par][:, a, :, R_MASK:R_MASK + 4],
                                     query_mask[:, a, :].unsqueeze(1).broadcast_to([P, HEADS, 4])).then_inc(s_stack0, 1)
                pool.tensor_copy(k_stack[par][:, :, :],
                                 key_rows[:, :].unsqueeze(1).broadcast_to([P, HEADS, TOK])).then_inc(s_stack0, 1)

            def rstd(i, n):
                pool.wait_ge(n_var[i], n + 1)
                pool.wait_ge(n_hat[i], n)
                settle(pool, n)
                pool.tensor_tensor(norm_rstd[i][:, :], norm_var[i][:, :], minus_half[:, :],
                                   ALU.pow).then_inc(n_rstd[i], 1)

            def add_bias(L, n, bias, done):
                xs = x_slot(IMAGES * L, n)
                pool.tensor_tensor(xs, xs, bias[:, :].unsqueeze(1).broadcast_to([P, TILES, D]),
                                   ALU.add).then_inc(done, 1)

            def split_weights(L):
                pool.wait_ge(s_wx, 48 * (L + 1))
                pool.tensor_scalar(wqkv_in[:, :, D:2 * D], wqkv_in[:, :, D:2 * D], HD ** -0.5, None,
                                   ALU.mult).then_inc(s_wxs, 1)
                pool.wait_ge(s_wxs, L + 1)
                pool.wait_ge(s_qkv, 3 * IMAGES * L)
                pool.tensor_copy(wqkv_hi[:, :, :], wqkv_in[:, :, :]).then_inc(s_wxh, 1)
                pool.wait_ge(s_wxh, L + 1)
                pool.tensor_tensor(wqkv_lo[:, :, :], wqkv_in[:, :, :], wqkv_hi[:, :, :].bitcast(F32),
                                   ALU.subtract).then_inc(s_wxl, 1)

            def split_w1(L):
                pool.wait_ge(s_wy, 48 * (L + 1))
                pool.wait_ge(s_f1, MC * IMAGES * L)
                pool.tensor_copy(w1_hi[:, :, :], w1_in[:, :, :]).then_inc(s_wyh, 1)
                pool.wait_ge(s_wyh, L + 1)
                pool.tensor_tensor(w1_lo[:, :, :], w1_in[:, :, :], w1_hi[:, :, :].bitcast(F32),
                                   ALU.subtract).then_inc(s_wyl, 1)

            def biases_and_pads(n, L, par, t):
                if t == -11 and peeled(n) and n < 2:
                    constant_rows(n)
                if t == -12 and peeled(n) and n == IMAGES:
                    split_weights(1)
                if t == 24 and peeled(n) and n == IMAGES:
                    split_w1(1)
                if t == 0:
                    pool.wait_ge(n_hat[0], n + 1)
                    pool.wait_ge(s_w, W_LOADS)
                    settle(pool, n)
                    add_bias(L, n, pb[L], s_xb)
                if t == 1:
                    pool.wait_ge(s_pmax, n + 1)
                    pool.wait_ge(s_psum, n)
                    settle(pool, n)
                    for a in range(TILES):
                        src = rel_tok[:, a, 0:2 * HEADS * WS].rearrange("p (h k) -> p h k", k=WS)
                        dst = pad_e[:, a * 2 * HEADS:(a + 1) * 2 * HEADS, :]
                        for s, (lo, hi) in enumerate(((0, EDGE), (EDGE, WS))):
                            m = seg_max[s][:, a, :, :].rearrange("p w h -> p (w h)").unsqueeze(2)
                            last = pool.tensor_tensor(dst[:, :, lo:hi], src[:, :, lo:hi],
                                                      m.broadcast_to([P, 2 * HEADS, hi - lo]), ALU.subtract)
                    last.then_inc(s_psub, 1)
                if t == 2:
                    pool.wait_ge(s_qkvo, 3 * (n + 1))
                    if from_second(n):
                        pool.wait_ge(s_av, HEADS * (n - 1))
                    settle(pool, n)
                    pool.tensor_copy(v_ones[par][:, :, :, 0:HD],
                                     v_new[:, :, :].rearrange("p a (h c) -> p a h c", c=HD)).then_inc(s_v, 1)
                if t == 4:
                    pool.wait_ge(s_psum, n + 1)
                    pool.wait_ge(s_wsub, n)
                    pool.wait_ge(s_wmul, n)
                    settle(pool, n)
                    for seg, (hs, ws) in enumerate(((0, 1), (1, 1), (1, 0))):
                        pool.tensor_tensor(pad_max[:, seg, :, :], seg_max[hs][:, :, 0, :], seg_max[ws][:, :, 1, :],
                                           ALU.add)
                        last = pool.tensor_tensor(pad_prod[:, seg, :, :], seg_sum[hs][:, :, 0, :],
                                                  seg_sum[ws][:, :, 1, :], ALU.mult)
                    last.then_inc(s_pcomb, 1)
                if t == 5:
                    pool.wait_ge(s_pcomb, n + 1)
                    settle(pool, n)
                    flat = pad_max[:, :, :, :].rearrange("p s a h -> p s (a h)")
                    pool.tensor_tensor(flat, flat, pad_mask[:, :, :], ALU.add).then_inc(s_pmask, 1)
                    pool.wait_ge(s_pmask, n + 1)
                    settle(pool, n)
                    pool.tensor_tensor(pad_max[:, :, :, :], pad_max[:, :, :, :],
                                       rel_tok[:, :, 2 * HEADS * WS:RW].unsqueeze(1).broadcast_to(
                                           [P, NSEG, TILES, HEADS]), ALU.add).then_inc(s_pqb, 1)
                if t == 13:
                    pool.wait_ge(s_top, n + 1)
                    pool.wait_ge(s_padsum, n)
                    settle(pool, n)
                    pool.tensor_tensor(pad_w[:, :, :], pad_max[:, :, :, :].rearrange("p s a h -> p s (a h)"),
                                       top[:, :, :].rearrange("p a h -> p (a h)").unsqueeze(1).broadcast_to(
                                           [P, NSEG, TILES * HEADS]), ALU.subtract).then_inc(s_wsub, 1)
                if t == 15:
                    pool.wait_ge(s_wexp, n + 1)
                    settle(pool, n)
                    pool.tensor_tensor(pad_w[:, :, :], pad_w[:, :, :],
                                       pad_prod[:, :, :, :].rearrange("p s a h -> p s (a h)"),
                                       ALU.mult).then_inc(s_wmul, 1)
                if t == 17:
                    pool.wait_ge(s_wmul, n + 1)
                    pool.wait_ge(s_n1, n)
                    pool.wait_ge(s_padout, n)
                    settle(pool, n)
                    sums = pad_sum[:, :, :].rearrange("p a h -> p (a h)")
                    pool.tensor_tensor(sums, pad_w[:, 0, :], pad_w[:, 1, :], ALU.add).then_inc(s_padhalf, 1)
                    pool.wait_ge(s_padhalf, n + 1)
                    settle(pool, n)
                    pool.tensor_tensor(sums, sums, pad_w[:, 2, :], ALU.add).then_inc(s_padsum, 1)
                if t == 18:
                    pool.wait_ge(s_padsum, n + 1)
                    pool.wait_ge(s_n1, n)
                    settle(pool, n)
                    for a in range(TILES):
                        last = pool.tensor_tensor(
                            pad_out[:, a, :, :],
                            qkvb[L][:, 2 * D:QKV].rearrange("p (h c) -> p h c", c=HD),
                            pad_sum[:, a, :].unsqueeze(2).broadcast_to([P, HEADS, HD]), ALU.mult)
                    last.then_inc(s_padout, 1)
                if t == 31:
                    pool.wait_ge(n_hat[1], n + 1)
                    settle(pool, n)
                    add_bias(L, n, b2[L], s_xb2)

            def roots(n, L, par, t):
                if t == -12:
                    rstd(0, n)
                if t == 29:
                    rstd(1, n)

            run(pool, biases_and_pads, roots)

        @block.scalar
        def _(act):
            act.wait_ge(s_wxs, 1)
            act.wait_ge(s_zero, ZEROED)
            act.activation(wqkv_hi[:, :, :], wqkv_in[:, :, :], ACT.Copy).then_inc(s_wxh, 1)

            def affine(i, n, L, bank):
                act.wait_ge(n_tr[i], n + 1)
                act.wait_ge(n_hi[i], n)
                act.wait_ge(n_lo[i], n)
                act.wait_ge(s_vec, V_LOADS)
                norm = (n1, n2)[i][L]
                for c in range(2):
                    last = act.activation(xn[i][:, c, :], bank[:, c * TOK:(c + 1) * TOK], ACT.Identity,
                                          bias=norm[:, c, 1:2], scale=norm[:, c, 0:1])
                last.then_inc(n_aff[i], 1)

            def exps(n, L, par, t):
                h = t - 14
                if 0 <= h < HEADS:
                    act.wait_ge(s_st, HEADS * n + h + 1)
                    if not (peeled(n) and n == 0) or h >= NP:
                        act.wait_ge(s_av, HEADS * n + h - NP + 1)
                    act.activation(probs[h % NP][:, :, :], KB[h % 2][:, :].rearrange("p (k t) -> p k t", k=2),
                                   ACT.Exp).then_inc(s_ex, 1)

            def chain(n, L, par, t):
                if t == -10:
                    affine(0, n, L, FB)
                if t == -5:
                    act.wait_ge(s_qt, n + 1)
                    act.wait_ge(s_rel, 2 * n)
                    act.wait_ge(s_rt, TILES * n)
                    act.activation(q_t[:, :, :], FB[0:GF, :].rearrange("p (g t) -> p g t", g=2),
                                   ACT.Copy).then_inc(s_qto, 1)
                if t in (-4, -3):
                    w = t + 4
                    act.wait_ge(s_rel, 2 * n + w + 1)
                    act.wait_ge(s_rt, TILES * n)
                    act.activation(rel_t[:, w, :, :].rearrange("p g (r c) -> p g r c", c=SIDE),
                                   FB[0:GR, :].rearrange("p (g r c) -> p g r c" if w == 0 else "p (g c r) -> p g r c",
                                                         g=2, r=SIDE), ACT.Copy).then_inc(s_relo, 1)
                if t in (-2, -1):
                    a = t + 2
                    if a == 0:
                        act.wait_ge(s_pqb, n)
                        act.wait_ge(s_rlo, TILES * n)
                        act.wait_ge(s_psub, n)
                    act.wait_ge(s_rt, TILES * n + a + 1)
                    act.activation(rel_tok[:, a, 0:4 * GR].rearrange("p (x h k) -> p x h k", h=GH, k=WS),
                                   FB[:, 0:4 * GR].rearrange("p (x k h) -> p x h k", h=GH, k=WS), ACT.Copy)
                    act.activation(rel_tok[:, a, 4 * GR:RW], FB[:, 4 * GR:RW], ACT.Copy).then_inc(s_rto, 1)
                if t == 2:
                    act.wait_ge(s_psub, n + 1)
                    act.activation(pad_e[:, :, :], pad_e[:, :, :], ACT.Exp).then_inc(s_pexp, 1)
                if t == 14:
                    act.wait_ge(s_wsub, n + 1)
                    act.activation(pad_w[:, :, :], pad_w[:, :, :], ACT.Exp).then_inc(s_wexp, 1)
                if t == 3 and peeled(n) and n == 0:
                    act.wait_ge(s_wy, 48)
                    act.activation(w1_hi[:, :, :], w1_in[:, :, :], ACT.Copy).then_inc(s_wyh, 1)
                if t == 28:
                    act.wait_ge(s_at, n + 1)
                    act.wait_ge(s_pr, n)
                    act.activation(att_t[:, 0, :], BB[0][:, 0:TOK], ACT.Copy)
                    act.activation(att_t[0:LO, 1, :], BB[0][0:LO, TOK:2 * TOK], ACT.Copy).then_inc(s_ato, 1)
                if t == 31:
                    affine(1, n, L, BB[0])
                if t == 33:
                    for m in range(MC):
                        act.wait_ge(s_f1, MC * n + 2 * (m // 2) + 2)
                        act.wait_ge(s_f2, TILES * n)
                        act.activation(hid[:, m, :], fc1_psum(m), ACT.Gelu,
                                       bias=b1[L][:, m:m + 1]).then_inc(s_ge, 1)

            def stacks(n, L, par, t):
                if 0 <= t < HEADS and not STACK_ON_DVE[t]:
                    h = t
                    act.wait_ge(s_tr, HEADS * n + h + 1)
                    act.wait_ge(s_stack0, STACK_SETUP)
                    if from_second(n):
                        act.wait_ge(s_st, HEADS * (n - 2) + h + 1)
                    act.activation(q_stack[par][:, h, :], TB[:, 0:TOK], ACT.Copy)
                    act.activation(k_stack[par][0:KROWS, h, :], TB[0:KROWS, TOK:2 * TOK],
                                   ACT.Copy).then_inc(s_sta, 1)
                if t == 13:
                    act.wait_ge(s_nt, n + 1)
                    act.wait_ge(s_nd, 32 * n)
                    act.activation(neg_top_t[:, :], BB[1][0:2 * HEADS, 0:TOK], ACT.Copy).then_inc(s_nto, 1)

            run(act, exps, chain, stacks)

        @block.vector
        def _(dve):
            for par in range(2):
                dve.memset(q_stack_tok[par][:, :, :, :].bitcast(F32), 0.0).then_inc(s_zero, 1)
            dve.wait_ge(s_wx, 48)
            dve.tensor_scalar(wqkv_in[:, :, D:2 * D], wqkv_in[:, :, D:2 * D], HD ** -0.5, None,
                              ALU.mult).then_inc(s_wxs, 1)

            def setup_vectors():
                dve.wait_ge(s_vec, V_LOADS)
                dve.wait_ge(s_const, 16 * len(CONSTS))
                for l in range(2):
                    dve.tensor_scalar(qkvb[l][:, D:2 * D], qkvb[l][:, D:2 * D], HD ** -0.5, None,
                                      ALU.mult).then_inc(s_setup, 1)
                    dve.tensor_scalar(kb[l], kb[l], HD ** -0.5, None, ALU.mult).then_inc(s_kb, 1)
                    dve.wait_ge(s_kb, l + 1)
                    dve.tensor_tensor(kb_blocks[l][:, :, :],
                                      head_mask[:, :].unsqueeze(1).broadcast_to([GF, 2, GH]),
                                      kb[l].unsqueeze(2).broadcast_to([GF, 2, GH]),
                                      ALU.mult).then_inc(s_setup, 1)
                    offsets = 2 * (2 * WS - 1)
                    dve.tensor_tensor(
                        rel_heads[l][:, :, :, :].rearrange("p w o h -> p (w o) h"),
                        rel[l][:, :, :].rearrange("p w o -> p (w o)").unsqueeze(2).broadcast_to([GF, offsets, GH]),
                        head_mask[:, :].unsqueeze(1).broadcast_to([GF, offsets, GH]), ALU.mult).then_inc(s_setup, 1)

            def norm_stats(i, n, L):
                xs = x_slot(IMAGES * L, n)
                dve.wait_ge(n_aggr[i], n)
                settle(dve, n)
                for a in range(TILES):
                    last = dve.bn_stats(norm_s[i][:, a, :], xs[:, a, :])
                last.then_inc(n_stat[i], 1)
                dve.wait_ge(n_stat[i], n + 1)
                dve.wait_ge(n_hat[i], n)
                settle(dve, n)
                for a in range(TILES):
                    last = dve.bn_aggr(norm_mv[i][:, a, :], norm_s[i][:, a, :])
                last.then_inc(n_aggr[i], 1)
                dve.wait_ge(n_aggr[i], n + 1)
                dve.wait_ge(n_rstd[i], n)
                dve.tensor_scalar(norm_var[i][:, :], norm_mv[i][:, :, 1], EPS[L], None, ALU.add).then_inc(n_var[i], 1)

            def norm_hat(i, n, L):
                xs = x_slot(IMAGES * L, n)
                dve.wait_ge(n_rstd[i], n + 1)
                dve.wait_ge(n_tr[i], n)
                for a in range(TILES):
                    mean, r = norm_mv[i][:, a, 0:1], norm_rstd[i][:, a:a + 1]
                    dve.tensor_scalar(xhat[i][:, a, 0:P], xs[:, a, 0:P], mean, r, ALU.subtract, ALU.mult)
                    last = dve.tensor_scalar(
                        xhat[i][:, a, P:2 * P].rearrange("p (t f) -> p t f", t=2),
                        xs[:, a, P:D].unsqueeze(1).broadcast_to([P, 2, LO]), mean, r, ALU.subtract, ALU.mult)
                last.then_inc(n_hat[i], 1)

            def split_norm(i, n):
                dve.wait_ge(n_aff[i], n + 1)
                dve.wait_ge(s_qkv if i == 0 else s_f1, (3 if i == 0 else MC) * n)
                dve.tensor_copy(xn_hi[i][:, :, :], xn[i][:, :, :]).then_inc(n_hi[i], 1)
                dve.wait_ge(n_hi[i], n + 1)
                dve.tensor_tensor(xn_lo[i][:, :], xn[i][:, 0, :], xn_hi[i][:, 0, :].bitcast(F32), ALU.subtract)
                dve.tensor_tensor(xn_hi[i][LO:P, 1, :], xn[i][LO:P, 1, :], xn_hi[i][LO:P, 1, :].bitcast(F32),
                                  ALU.subtract).then_inc(n_lo[i], 1)

            def split_rel(n, par, a):
                dve.wait_ge(s_rto, TILES * n + a + 1)
                rows = q_stack_tok[par][:, a, :, R_RHI:R_RLO].rearrange("p h (w k) -> p w h k", w=2)
                low = q_stack_tok[par][:, a, :, R_RLO:R_MASK].rearrange("p h (w k) -> p w h k", w=2)
                src = rel_tok[:, a, 0:2 * HEADS * WS].rearrange("p (w h k) -> p w h k", w=2, k=WS)
                dve.tensor_copy(rows, src).then_inc(s_rhi, 1)
                dve.wait_ge(s_rhi, TILES * n + a + 1)
                dve.tensor_tensor(low, src, rows.bitcast(F32), ALU.subtract).then_inc(s_rlo, 1)

            def chain(n, L, par, t):
                if t == -11:
                    norm_hat(0, n, L)
                    if peeled(n) and n == 0:
                        setup_vectors()
                if t in (-8, -7):
                    a = t + 8
                    dve.wait_ge(s_qkv, 3 * n + a + 1)
                    dve.wait_ge(s_setup, SETUP_DVE)
                    if a == 0:
                        dve.wait_ge(s_qkh, n)
                        dve.wait_ge(s_qkl, n)
                        dve.wait_ge(s_qt, n)
                    dve.tensor_tensor(qk[:, a, :], FB[:, 0:2 * D], qkvb[L][:, 0:2 * D], ALU.add).then_inc(s_qkvo, 1)
                if t == -6:
                    dve.wait_ge(s_qkv, 3 * (n + 1))
                    dve.wait_ge(s_v, n)
                    dve.tensor_tensor(v_new[:, :, :],
                                      FB[:, :].rearrange("p (a f) -> p a f", a=TILES)[:, :, 0:D],
                                      qkvb[L][:, 2 * D:QKV].unsqueeze(1).broadcast_to([P, TILES, D]),
                                      ALU.add).then_inc(s_qkvo, 1)
                    dve.wait_ge(s_qkvo, 3 * (n + 1))
                    dve.wait_ge(s_zero, ZEROED)
                    if from_second(n):
                        dve.wait_ge(s_tr, HEADS * (n - 1))
                    for a in range(TILES):
                        dve.tensor_copy(
                            q_stack_tok[par][:, a, :, 0:2 * HD].rearrange("p h (t c) -> p h t c", t=2),
                            qk[:, a, 0:D].rearrange("p (h c) -> p h c", c=HD).unsqueeze(2)
                            .broadcast_to([P, HEADS, 2, HD]))
                    k_in = qk[:, :, D:2 * D].rearrange("p a (h c) -> p a h c", c=HD)
                    for at in (0, 2 * HD):
                        last = dve.tensor_copy(k_stack_tok[par][:, :, :, at:at + HD], k_in)
                    last.then_inc(s_qkh, 1)
                if t == -5:
                    dve.wait_ge(s_qkh, n + 1)
                    dve.tensor_tensor(
                        q_stack_tok[par][:, :, :, R_QLO:R_QLO + HD],
                        qk[:, :, 0:D].rearrange("p a (h c) -> p a h c", c=HD),
                        q_stack_tok[par][:, :, :, 0:HD].bitcast(F32), ALU.subtract)
                    dve.tensor_tensor(
                        k_stack_tok[par][:, :, :, HD:2 * HD],
                        qk[:, :, D:2 * D].rearrange("p a (h c) -> p a h c", c=HD),
                        k_stack_tok[par][:, :, :, 0:HD].bitcast(F32), ALU.subtract).then_inc(s_qkl, 1)
                if t == -1:
                    split_rel(n, par, 0)
                if t == 0:
                    dve.wait_ge(s_rto, TILES * (n + 1))
                    dve.wait_ge(s_psub, n)
                    dve.wait_ge(s_pcomb, n)
                    rows = rel_tok[:, :, 0:2 * HEADS * WS].rearrange("p a (h k) -> p a h k", k=WS)
                    for s, (lo, hi) in enumerate(((0, EDGE), (EDGE, WS))):
                        last = dve.tensor_reduce(seg_max[s][:, :, :, :].rearrange("p a w h -> p a (w h)"),
                                                 rows[:, :, :, lo:hi], AX, ALU.max)
                    last.then_inc(s_pmax, 1)
                if t == 3:
                    dve.wait_ge(s_pexp, n + 1)
                    dve.wait_ge(s_pcomb, n)
                    for s, (lo, hi) in enumerate(((0, EDGE), (EDGE, WS))):
                        last = dve.tensor_reduce(
                            seg_sum[s][:, :, :, :].rearrange("p a w h -> p (a w h)"), pad_e[:, :, lo:hi], AX, ALU.add)
                    last.then_inc(s_psum, 1)
                if t == 7:
                    dve.wait_ge(s_pqb, n + 1)
                    dve.wait_ge(s_top, n)
                    dve.tensor_reduce(pad_top[:, :], pad_max[:, :, :, :].rearrange("p s a h -> p (a h) s"), AX,
                                      ALU.max).then_inc(s_ptop, 1)
                if t == 27:
                    dve.wait_ge(s_av, HEADS * (n + 1))
                    dve.wait_ge(s_padout, n + 1)
                    dve.wait_ge(s_padsum, n + 1)
                    dve.wait_ge(s_at, n)
                    dve.wait_ge(s_att, n)
                    o = VB[:, :].rearrange("p (a t) -> p a t", a=TILES)[:, :, 0:HEADS * VW] \
                        .rearrange("p a (h c) -> p a h c", c=VW)
                    a4 = att[:, :, :].rearrange("p a (h c) -> p a h c", c=HD)
                    dve.tensor_tensor(a4, o[:, :, :, 0:HD], pad_out[:, :, :, :], ALU.add)
                    dve.tensor_tensor(den[:, :, :], o[:, :, :, HD], pad_sum[:, :, :], ALU.add).then_inc(s_n1, 1)
                    dve.wait_ge(s_n1, n + 1)
                    dve.reciprocal(den[:, :, :], den[:, :, :]).then_inc(s_n2, 1)
                    dve.wait_ge(s_n2, n + 1)
                    dve.tensor_tensor(a4, a4, den[:, :, :].unsqueeze(3).broadcast_to([P, TILES, HEADS, HD]),
                                      ALU.mult).then_inc(s_att, 1)
                if t == 29:
                    xs = x_slot(IMAGES * L, n)
                    dve.wait_ge(s_pr, n + 1)
                    dve.wait_ge(s_xb, n + 1)
                    dve.tensor_tensor(xs, xs, BB[1][:, 0:TILES * D].rearrange("p (a d) -> p a d", d=D),
                                      ALU.add).then_inc(s_xa, 1)
                    dve.wait_ge(s_xa, n + 1)
                    norm_stats(1, n, L)
                if t == 30:
                    norm_hat(1, n, L)

            def row_maxima(n, L, par, t):
                if 0 <= t < HEADS and STACK_ON_DVE[t]:
                    dve.wait_ge(s_tr, HEADS * n + t + 1)
                    dve.wait_ge(s_stack0, STACK_SETUP)
                    if from_second(n):
                        dve.wait_ge(s_st, HEADS * (n - 2) + t + 1)
                    dve.tensor_copy(q_stack[par][:, t, :], TB[:, 0:TOK])
                    dve.tensor_copy(k_stack[par][0:KROWS, t, :], TB[0:KROWS, TOK:2 * TOK]).then_inc(s_std, 1)
                h = t - 1
                if 0 <= h < HEADS:
                    dve.wait_ge(s_s, HEADS * n + h + 1)
                    if h == 0:
                        dve.wait_ge(s_top, n)
                    dve.tensor_reduce(row_max[:, h, :], QB[:, :].rearrange("p (a t) -> p a t", a=TILES), AX,
                                      ALU.max).then_inc(s_smax, 1)

            def chain_end(n, L, par, t):
                if t == -12:
                    if peeled(n) and n == 0:
                        dve.wait_ge(s_x0, 16)
                    else:
                        dve.wait_ge(s_x, 16)
                    if L == 1:
                        dve.wait_ge(s_xm, n - IMAGES + 1)
                    norm_stats(0, n, L)
                if t == -10:
                    split_norm(0, n)
                    if peeled(n) and n == 0:
                        dve.wait_ge(s_wxh, 1)
                        dve.tensor_tensor(wqkv_lo[:, :, :], wqkv_in[:, :, :], wqkv_hi[:, :, :].bitcast(F32),
                                          ALU.subtract).then_inc(s_wxl, 1)
                if t == -1:
                    split_rel(n, par, 1)
                if t == 12:
                    dve.wait_ge(s_smax, HEADS * (n + 1))
                    dve.wait_ge(s_ptop, n + 1)
                    dve.wait_ge(s_nlo, n)
                    dve.wait_ge(s_wsub, n)
                    dve.tensor_tensor(top[:, :, :], row_max[:, :, :].rearrange("p h a -> p a h"),
                                      pad_top[:, :].rearrange("p (a h) -> p a h", a=TILES), ALU.max).then_inc(s_top, 1)
                    dve.wait_ge(s_top, n + 1)
                    dve.wait_ge(s_nt, n)
                    dve.tensor_scalar(neg_top[:, :, 0, :], top[:, :, :], -1.0, None, ALU.mult).then_inc(s_nhi, 1)
                    dve.wait_ge(s_nhi, n + 1)
                    dve.scalar_tensor_tensor(neg_top[:, :, 1, :], top[:, :, :], -1.0, neg_top[:, :, 0, :].bitcast(F32),
                                             ALU.mult, ALU.subtract).then_inc(s_nlo, 1)
                if t == 4 and peeled(n) and n == 0:
                    dve.wait_ge(s_wyh, 1)
                    dve.tensor_tensor(w1_lo[:, :, :], w1_in[:, :, :], w1_hi[:, :, :].bitcast(F32),
                                      ALU.subtract).then_inc(s_wyl, 1)
                if t == 31:
                    split_norm(1, n)
                if t == 35:
                    xs = x_slot(IMAGES * L, n)
                    dve.wait_ge(s_f2, TILES * (n + 1))
                    dve.wait_ge(s_xb2, n + 1)
                    dve.tensor_tensor(xs, xs, BB[0][:, 0:TILES * D].rearrange("p (a d) -> p a d", d=D),
                                      ALU.add).then_inc(s_xm, 1)

            run(dve, chain, row_maxima, chain_end)

        @block.tensor
        def _(pe):
            def split_product(psum, chunks):
                for i, (lhs, rhs) in enumerate(chunks):
                    last = pe.matmul(psum, lhs, rhs, start=(i == 0), stop=(i == len(chunks) - 1))
                return last

            def norm_transposes(i, n, bank):
                pe.wait_ge(n_hat[i], n + 1)
                for c in range(2):
                    for a in range(TILES):
                        last = pe.transpose(bank[:, c * TOK + a * P:c * TOK + (a + 1) * P],
                                            xhat[i][:, a, c * P:(c + 1) * P], ident[:, :])
                last.then_inc(n_tr[i], 1)

            def xn_times(psum, a, cols):
                tok = slice(a * P, (a + 1) * P)
                return split_product(psum, [
                    (xn_hi[0][:, 0, tok], wqkv_hi[:, 0, cols]), (xn_hi[0][:, 0, tok], wqkv_lo[:, 0, cols]),
                    (xn_lo[0][:, tok], wqkv_hi[:, 0, cols]),
                    (xn_hi[0][:, 1, tok], wqkv_hi[:, 1, cols]), (xn_hi[0][:, 1, tok], wqkv_lo[:, 1, cols])])

            def front(n, L, par, t):
                if t == -11:
                    pe.wait_ge(s_rto, TILES * n)
                    pe.wait_ge(s_const, 16 * len(CONSTS))
                    norm_transposes(0, n, FB)
                if t in (-9, -8):
                    a = t + 9
                    if a == 0:
                        pe.wait_ge(n_lo[0], n + 1)
                        pe.wait_ge(s_wxl, L + 1)
                        pe.wait_ge(n_aff[0], n + 1)
                    else:
                        pe.wait_ge(s_qkvo, 3 * n + 1)
                    xn_times(FB[:, 0:2 * D], a, slice(0, 2 * D)).then_inc(s_qkv, 1)
                if t == -7:
                    pe.wait_ge(s_qkvo, 3 * n + 2)
                    for a in range(TILES):
                        last = xn_times(FB[:, a * TOK:(a + 1) * TOK], a, slice(2 * D, WCOLS))
                    last.then_inc(s_qkv, 1)
                if t == -6:
                    pe.wait_ge(s_qkvo, 3 * (n + 1))
                    for g in range(2):
                        for a in range(TILES):
                            last = pe.transpose(FB[0:GF, g * TOK + a * P:g * TOK + (a + 1) * P],
                                                qk[:, a, g * GF:(g + 1) * GF], ident[:, :])
                    last.then_inc(s_qt, 1)
                if t in (-5, -4):
                    w = t + 5
                    if w == 0:
                        pe.wait_ge(s_qto, n + 1)
                        pe.wait_ge(s_setup, SETUP_DVE)
                    else:
                        pe.wait_ge(s_relo, 2 * n + 1)
                    grid = q_t[:, :, :].rearrange("p g (r c) -> p g r c" if w == 0 else "p g (r c) -> p g c r", c=SIDE)
                    dst = FB[0:GR, :].rearrange("p (g r c) -> p g r c", g=2, c=SIDE)
                    for i in range(WS):
                        at = slice(i, i + WS + 1, WS) if i < EDGE else slice(i, i + 1)
                        last = pe.matmul(dst[:, :, at, :], rel_heads[L][:, w, WS - 1 - i:2 * WS - 1 - i, :]
                                         .rearrange("p k h -> p (k h)"), grid[:, :, at, :], start=True, stop=True)
                    last.then_inc(s_rel, 1)
                if t in (-3, -2):
                    a = t + 3
                    if a == 0:
                        pe.wait_ge(s_relo, 2 * (n + 1))
                    else:
                        pe.wait_ge(s_rto, TILES * n + 1)
                    for w in range(2):
                        for g in range(2):
                            col = (w * 2 + g) * GR
                            pe.transpose(FB[:, col:col + GR], rel_t[:, w, g, a * P:(a + 1) * P],
                                         ident[0:GR, 0:GR])
                    for g in range(2):
                        col = 4 * GR + g * GH
                        last = pe.matmul(FB[:, col:col + GH], q_t[:, g, a * P:(a + 1) * P],
                                         kb_blocks[L][:, g, :], start=True, stop=True)
                    last.then_inc(s_rt, 1)

            def scores_by_key(n, L, par, t):
                h = t - 14
                if 0 <= h < HEADS:
                    if h == 0:
                        pe.wait_ge(s_nd, 32 * (n + 1))
                    if not (peeled(n) and n == 0) or h >= 2:
                        pe.wait_ge(s_ex, HEADS * n + h - 1)
                    for c in range(2):
                        last = pe.matmul(KB[h % 2][:, c * TOK:(c + 1) * TOK], k_stack[par][:, h, c * P:(c + 1) * P],
                                         q_stack[par][:, h, :], start=True, stop=True)
                    last.then_inc(s_st, 1)

            def times_v(n, L, par, t):
                h = t - 15
                if 0 <= h < HEADS:
                    if h == 0:
                        pe.wait_ge(s_n1, n)
                        pe.wait_ge(s_v, n + 1)
                    pe.wait_ge(s_ex, HEADS * n + h + 1)
                    for a in range(TILES):
                        for c in range(2):
                            last = pe.matmul(VB[:, a * TOK + h * VW:a * TOK + (h + 1) * VW],
                                             probs[h % NP][:, c, a * P:(a + 1) * P], v_ones[par][:, c, h, :],
                                             start=(c == 0), stop=(c == 1))
                    last.then_inc(s_av, 1)

            def evacuated(n, h):
                by_dve = sum(STACK_ON_DVE[:h + 1])
                if STACK_ON_DVE[h]:
                    pe.wait_ge(s_std, sum(STACK_ON_DVE) * n + by_dve)
                else:
                    pe.wait_ge(s_sta, (HEADS - sum(STACK_ON_DVE)) * n + h + 1 - by_dve)

            def stacks(n, L, par, t):
                h = t - 1
                if 0 <= h < HEADS:
                    evacuated(n, h)
                    if not (peeled(n) and n == 0 and h == 0):
                        pe.wait_ge(s_smax, HEADS * n + h)
                    for a in range(TILES):
                        last = pe.matmul(QB[:, a * TOK:(a + 1) * TOK], q_stack[par][:, h, a * P:(a + 1) * P],
                                         k_stack[par][:, h, :], start=True, stop=True)
                    last.then_inc(s_s, 1)

            def transposes(n, L, par, t):
                h = t
                if 0 <= h < HEADS:
                    if h == 0:
                        pe.wait_ge(s_qkl, n + 1)
                        pe.wait_ge(s_qkh, n + 1)
                        pe.wait_ge(s_rlo, TILES * (n + 1))
                        pe.wait_ge(s_rhi, TILES * (n + 1))
                        pe.wait_ge(s_stack0, STACK_SETUP)
                        if from_second(n):
                            evacuated(n - 1, HEADS - 1)
                        elif n == 1:
                            evacuated(0, HEADS - 1)
                    else:
                        evacuated(n, h - 1)
                    for a in range(TILES):
                        pe.transpose(TB[:, a * P:(a + 1) * P], q_stack_tok[par][:, a, h, :].bitcast(F32), ident[:, :])
                    settle(pe, n)
                    for a in range(TILES):
                        last = pe.transpose(TB[0:KROWS, TOK + a * P:TOK + (a + 1) * P],
                                            k_stack_tok[par][:, a, h, :].bitcast(F32), ident[:, :])
                    last.then_inc(s_tr, 1)
                if t == 13:
                    pe.wait_ge(s_nlo, n + 1)
                    pe.wait_ge(s_nhi, n + 1)
                    if from_second(n):
                        pe.wait_ge(s_ge, MC * (n - 1))
                    for a in range(TILES):
                        last = pe.transpose(BB[1][0:2 * HEADS, a * P:(a + 1) * P],
                                            neg_top[:, a, :, :].rearrange("p t h -> p (t h)").bitcast(F32), ident[:, :])
                    last.then_inc(s_nt, 1)

            def fc1(n, L, m):
                f = slice(m * P, (m + 1) * P)
                split_product(fc1_psum(m), [
                    (w1_hi[:, 0, f], xn_hi[1][:, 0, :]), (w1_lo[:, 0, f], xn_hi[1][:, 0, :]),
                    (w1_hi[:, 0, f], xn_lo[1][:, :]),
                    (w1_hi[:, 1, f], xn_hi[1][:, 1, :]), (w1_lo[:, 1, f], xn_hi[1][:, 1, :])]).then_inc(s_f1, 1)

            def back(n, L, par, t):
                if t == 27:
                    pe.wait_ge(s_att, n + 1)
                    pe.wait_ge(s_xm, n)
                    for a in range(TILES):
                        pe.transpose(BB[0][:, a * P:(a + 1) * P], att[:, a, 0:P], ident[:, :])
                        last = pe.transpose(BB[0][0:LO, TOK + a * P:TOK + (a + 1) * P], att[:, a, P:D], ident[:, :])
                    last.then_inc(s_at, 1)
                if t == 28:
                    pe.wait_ge(s_ato, n + 1)
                    pe.wait_ge(s_w, W_LOADS)
                    pe.wait_ge(s_nto, min(n + 2, 2 * IMAGES) if peeled(n) else n + 2)
                    for a in range(TILES):
                        last = split_product(BB[1][:, a * D:(a + 1) * D], [
                            (att_t[:, 0, a * P:(a + 1) * P], wp[L][:, 0, :]),
                            (att_t[0:LO, 1, a * P:(a + 1) * P], wp[L][0:LO, 1, :])])
                    last.then_inc(s_pr, 1)
                if t == 30:
                    pe.wait_ge(s_ato, n + 1)
                    norm_transposes(1, n, BB[0])
                if t == 32:
                    pe.wait_ge(n_lo[1], n + 1)
                    pe.wait_ge(s_wyl, L + 1)
                    pe.wait_ge(s_xa, n + 1)
                    pe.wait_ge(n_aff[1], n + 1)
                    for m in range(4):
                        fc1(n, L, m)
                if t == 33:
                    pe.wait_ge(s_ge, MC * n + 2)
                    for m in range(4, MC):
                        fc1(n, L, m)
                if t in (34, 35):
                    a = t - 34
                    for m in range(MC):
                        if a == 0:
                            pe.wait_ge(s_ge, MC * n + max(m + 1, 4))
                        last = pe.matmul(BB[0][:, a * D:(a + 1) * D], hid[:, m, a * P:(a + 1) * P], w2[L][:, m, :],
                                         start=(m == 0), stop=(m == MC - 1))
                    last.then_inc(s_f2, 1)

            run(pe, scores_by_key, stacks, transposes, times_v, back, front)


def kernel(**inputs):
    import numpy as np
    import concourse.bacc as bacc
    from concourse.bass_utils import run_bass_kernel_spmd

    nc = bacc.Bacc("TRN2", target_bir_lowering=False, num_devices=1)
    arrays = {}

    def dram(name, a):
        a = np.ascontiguousarray(a)
        arrays[name] = a
        return nc.dram_tensor(name, a.shape, mybir.dt.from_np(a.dtype), kind="ExternalInput").ap()

    names = [dict(qkv_w="L0_conv_qkv_w", qkv_b="L0_conv_qkv_b", proj_w="L0_conv_proj_w", proj_b="L0_conv_proj_b",
                  rel_h="L0_conv_rel_pos_h", rel_w="L0_conv_rel_pos_w", n1_w="L0_conv_norm1_w",
                  n1_b="L0_conv_norm1_b", n2_w="L0_conv_norm2_w", n2_b="L0_conv_norm2_b", fc1_w="L0_conv_fc1_w",
                  fc1_b="L0_conv_fc1_b", fc2_w="L0_conv_fc2_w", fc2_b="L0_conv_fc2_b"),
             dict(qkv_w="L1_conv_w_qkv", qkv_b="L1_conv_b_qkv", proj_w="L1_conv_w_proj", proj_b="L1_conv_b_proj",
                  rel_h="L1_conv_rel_pos_h", rel_w="L1_conv_rel_pos_w", n1_w="L1_conv_ln1_g", n1_b="L1_conv_ln1_b",
                  n2_w="L1_conv_ln2_g", n2_b="L1_conv_ln2_b", fc1_w="L1_conv_w_fc1", fc1_b="L1_conv_b_fc1",
                  fc2_w="L1_conv_w_fc2", fc2_b="L1_conv_b_fc2")]
    x = dram("in_x", inputs["x"])
    layers = []
    for L, of in enumerate(names):
        layer = {k: dram(f"in_{k}_{L}", inputs[of[k]]) for k in LAYER_IN}
        columns = np.zeros((P, COLS), np.float32)
        for at, name in enumerate(("n1_w", "n1_b", "n2_w", "n2_b")):
            v, at = np.asarray(inputs[of[name]]), at + 2 * (at // 2)
            columns[:, at] = v[:P]
            columns[:, at + 2] = np.tile(v[P:], 2)
        columns[:, 8:8 + MC] = np.asarray(inputs[of["fc1_b"]]).reshape(MC, P).T
        columns[:GF, 8 + MC:] = np.asarray(inputs[of["qkv_b"]])[D:2 * D].reshape(2, GF).T
        layer["columns"] = dram(f"in_columns_{L}", columns)
        rels = [np.tile(np.asarray(inputs[of[r]])[::-1].T, (GH, 1)) for r in ("rel_h", "rel_w")]
        layer["rel"] = dram(f"in_rel_{L}", np.stack(rels, axis=1))
        layers.append(layer)

    r, c = np.divmod(np.arange(TOK), SIDE)
    window = 2 * (r >= WS) + (c >= WS)
    rows = np.zeros((P, TOK), np.float32)
    t = np.arange(TOK)
    for at in (R_RHI, R_RLO):
        rows[at + r % WS, t] = 1
        rows[at + WS + c % WS, t] = 1
    rows[R_MASK + window, t] = 1
    rows[R_MAX:R_MAX + 2] = 1
    w_tile = window.reshape(TILES, P).T
    q_mask = np.where(w_tile[:, :, None] == np.arange(4), 0, NEG).astype(np.float32)
    in_seg = np.stack([np.isin(w_tile, s) for s in ((1, 3), (1, 2, 3), (2, 3))], axis=1)
    p_mask = np.repeat(np.where(in_seg, 0, NEG)[:, :, :, None], HEADS, axis=3).reshape(P, NSEG, -1).astype(np.float32)
    h_mask = (np.arange(GF)[:, None] // HD == np.arange(GH)).astype(np.float32)
    const = {k: dram("c_" + k, a) for k, a in zip(CONSTS, (np.eye(P, dtype=np.float32), rows, q_mask, p_mask, h_mask))}

    out = nc.dram_tensor("out", (IMAGES, SIDE, SIDE, D), F32, kind="ExternalOutput").ap()
    build(nc, x, layers, const, out)
    r = run_bass_kernel_spmd(nc, [arrays], core_ids=[0])
    return r.results[0]["out"]
```

```python
from contextlib import ExitStack

import concourse.bass as bass
from concourse import mybir

F32 = mybir.dt.float32
F32R = mybir.dt.float32r
ALU = mybir.AluOpType
ACT = mybir.ActivationFunctionType
AX = mybir.AxisListType.X

P = 128
IMAGES, SIDE, D = 8, 16, 192
TOK = SIDE * SIDE
TILES = TOK // P
HEADS = 12
HD = D // HEADS
WS = 14
EDGE = SIDE - WS
MLP = 4 * D
MC = MLP // P
LO = D - P
QKV = 3 * D
WCOLS = 2 * D + 2 * P
GH = HEADS // 2
GF = GH * HD
GR = GH * WS
VW = 32
QUAD = P // VW
QUADS = HEADS // QUAD
NSEG = 3
NEG = -1.0e30
SETUP_DVE = 2 * 3
STACK_SETUP = TILES + 1
ZEROED = 2 + 4 + 1
COLS = 4 + 4 + MC + 2
C_LOADS = 16 * 4
V_LOADS = 16 * 2 * 2
W_LOADS = 16 * 2 * 5
STACK_ON_DVE = [h in (9, 10) for h in range(HEADS)]
EPS = (1e-5, 1e-6)

R_QLO, R_RHI, R_RLO, R_MASK, R_MAX = 2 * HD, 3 * HD, 3 * HD + 2 * WS, 3 * HD + 4 * WS, 3 * HD + 4 * WS + 4
KROWS = 3 * HD

LAYER_IN = ["qkv_w", "qkv_b", "proj_w", "proj_b", "fc1_w", "fc2_w", "fc2_b"]
CONSTS = ["ident", "key_rows", "query_mask", "pad_mask", "head_mask"]


def build(nc, x, layers, const, out):
    x_t = x.rearrange("b h w d -> (b h w) d").rearrange("(t p) d -> p t d", p=P)
    out_t = out.rearrange("b h w d -> (b h w) d").rearrange("(t p) d -> p t d", p=P)

    with ExitStack() as ctx:
        def sb(name, shape, dt=F32):
            return ctx.enter_context(nc.sbuf_tensor(name, shape, dt))

        def sem(name):
            return ctx.enter_context(nc.semaphore(name))

        X = sb("X", [P, IMAGES * TILES, D])
        ident = sb("ident", [P, P])
        query_mask = sb("query_mask", [P, TILES, 4])
        pad_mask = sb("pad_mask", [P, NSEG, TILES * HEADS])
        head_mask = sb("head_mask", [GF, GH])
        minus_half = sb("minus_half", [P, TILES])
        w1_in = sb("weights_in", [P, 2, MLP])
        wqkv_in = w1_in[:, :, 0:WCOLS]
        wqkv_hi, wqkv_lo = sb("wqkv_hi", [P, 2, WCOLS], F32R), sb("wqkv_lo", [P, 2, WCOLS], F32R)
        w1_hi, w1_lo = sb("w1_hi", [P, 2, MLP], F32R), sb("w1_lo", [P, 2, MLP], F32R)
        wp, w2, qkvb, pb, b2, columns, n1, n2, b1, rel, rel_heads, kb, kb_blocks = ([] for _ in range(13))
        for L in range(2):
            wp.append(sb(f"wp{L}", [P, 2, D]))
            w2.append(sb(f"w2{L}", [P, MC, D]))
            qkvb.append(sb(f"qkvb{L}", [P, QKV]))
            pb.append(sb(f"pb{L}", [P, D]))
            b2.append(sb(f"b2{L}", [P, D]))
            columns.append(sb(f"columns{L}", [P, COLS]))
            n1.append(columns[L][:, 0:4].rearrange("p (c w) -> p c w", c=2))
            n2.append(columns[L][:, 4:8].rearrange("p (c w) -> p c w", c=2))
            b1.append(columns[L][:, 8:8 + MC])
            rel_heads.append(sb(f"rel_heads{L}", [GF, 2, 2 * WS - 1, GH]))
            kb.append(columns[L][0:GF, 8 + MC:COLS])
            kb_blocks.append(sb(f"kb_blocks{L}", [GF, 2, GH]))
        norm_s = [sb(f"norm_s{i}", [P, TILES, 6]) for i in range(2)]
        norm_mv = [sb(f"norm_mv{i}", [P, TILES, 2]) for i in range(2)]
        norm_var = [sb(f"norm_var{i}", [P, TILES]) for i in range(2)]
        norm_rstd = [sb(f"norm_rstd{i}", [P, TILES]) for i in range(2)]
        xhat = [sb(f"xhat{i}", [P, TILES, 2 * P]) for i in range(2)]
        xn = [sb(f"xn{i}", [P, 2, TOK]) for i in range(2)]
        xn_hi = [sb(f"xn_hi{i}", [P, 2, TOK], F32R) for i in range(2)]
        xn_lo = [sb(f"xn_lo{i}", [P, TOK], F32R) for i in range(2)]
        qk = sb("qk", [P, TILES, 2 * D])
        q_t = sb("q_t", [GF, 2, TOK])
        rel_t = sb("rel_t", [GR, 2, 2, TOK])
        RW = 2 * HEADS * WS + HEADS
        rel_tok = sb("rel_tok", [P, TILES, RW])
        q_stack_tok = [sb(f"q_stack_tok{i}", [P, TILES, HEADS, P], F32R) for i in range(2)]
        k_stack_tok = [sb(f"k_stack_tok{i}", [P, TILES, HEADS, KROWS], F32R) for i in range(2)]
        v_new = sb("v_new", [P, TILES, D])
        q_stack = [sb(f"q_stack{i}", [P, HEADS, TOK], F32R) for i in range(2)]
        k_stack = [sb(f"k_stack{i}", [P, HEADS, TOK], F32R) for i in range(2)]
        v_ones = [sb(f"v_ones{i}", [P, TILES, HEADS, VW]) for i in range(2)]
        pad_e = sb("pad_e", [P, TILES * 2 * HEADS, WS])
        seg_max = [sb(f"seg_max{i}", [P, TILES, 2, HEADS]) for i in range(2)]
        seg_sum = [sb(f"seg_sum{i}", [P, TILES, 2, HEADS]) for i in range(2)]
        pad_max = sb("pad_max", [P, NSEG, TILES, HEADS])
        pad_prod = sb("pad_prod", [P, NSEG, TILES, HEADS])
        pad_top = sb("pad_top", [P, TILES * HEADS])
        pad_w = sb("pad_w", [P, NSEG, TILES * HEADS])
        row_max = sb("row_max", [P, HEADS, TILES])
        top = sb("top", [P, TILES, HEADS])
        neg_top = sb("neg_top", [P, TILES, 2, HEADS], F32R)
        neg_top_t = sb("neg_top_t", [2 * HEADS, TOK], F32R)
        pad_sum = sb("pad_sum", [P, TILES, HEADS])
        pad_out = sb("pad_out", [P, TILES, HEADS, HD])
        NP = 6
        probs = [sb(f"probs{i}", [P, 2, TOK]) for i in range(NP)]
        den = sb("den", [P, TILES, HEADS])
        att = sb("att", [P, TILES, D])
        for L in range(2):
            rel.append(att[0:GF, L, 0:2 * (2 * WS - 1)].rearrange("p (w o) -> p w o", w=2))
        av_t = sb("av_t", [P, QUADS, TOK])
        hid = sb("hid", [P, MC, TOK])
        att_t = hid[:, 0:2, :]
        key_rows = hid[:, 0, :]

        def bank(name):
            return ctx.enter_context(nc.psum_tensor(name, [P, 512], F32))

        FB = bank("front")
        TB, QB = bank("stack_transposes"), bank("by_query")
        KB = [bank(f"by_key{i}") for i in range(2)]
        VB = bank("times_v")
        BB = [bank(f"back{i}") for i in range(2)]

        def attention_psum(a, lo, hi):
            if lo < 2 * QUAD:
                b = BB[0][:, :].rearrange("p (a h c) -> p a h c", a=TILES, c=VW)
                return b[:, a, lo:hi, :]
            b = VB[:, TOK:2 * TOK].rearrange("p (a h c) -> p a h c", a=TILES, c=VW)
            return b[:, a, lo - 2 * QUAD:hi - 2 * QUAD, :]

        def fc1_psum(m):
            return BB[(1, 0, 1)[m // 2]][:, (m % 2) * TOK:(m % 2 + 1) * TOK]

        s_x0, s_x, s_const = sem("x0_loaded"), sem("x_loaded"), sem("const_loaded")
        s_vec, s_w, s_wx, s_wy = sem("vectors_loaded"), sem("weights_loaded"), sem("wqkv_loaded"), sem("w1_loaded")
        s_zero = sem("buffers_zeroed")
        s_id, s_col = sem("ident_loaded"), [sem(f"columns_loaded{L}") for L in range(2)]
        s_setup, s_stack0 = sem("vectors_ready"), sem("stack_constants_ready")
        s_kb = sem("k_bias_scaled")
        s_wxs, s_wxh, s_wxl = sem("wqkv_scaled"), sem("wqkv_hi_done"), sem("wqkv_lo_done")
        s_wyh, s_wyl = sem("w1_hi_done"), sem("w1_lo_done")
        n_stat = [sem(f"norm{i}_stats") for i in range(2)]
        n_aggr = [sem(f"norm{i}_aggregated") for i in range(2)]
        n_var = [sem(f"norm{i}_var") for i in range(2)]
        n_rstd = [sem(f"norm{i}_rstd") for i in range(2)]
        n_hat = [sem(f"norm{i}_hat") for i in range(2)]
        n_tr = [sem(f"norm{i}_transposed") for i in range(2)]
        n_aff = [sem(f"norm{i}_affine") for i in range(2)]
        n_hi = [sem(f"norm{i}_hi") for i in range(2)]
        n_lo = [sem(f"norm{i}_lo") for i in range(2)]
        s_qkv, s_qkvo = sem("qkv_product"), sem("qkv_biased")
        s_qt, s_qto = sem("q_transposed"), sem("q_t_ready")
        s_qkh, s_qkl = sem("qk_hi"), sem("qk_lo")
        s_rel, s_relo = sem("rel_product"), sem("rel_t_ready")
        s_rt, s_rto = sem("rel_transposed"), sem("rel_tok_ready")
        s_rhi, s_rlo = sem("rel_hi"), sem("rel_lo")
        s_v = sem("v_copied")
        s_pmax, s_psub, s_pexp = sem("pad_segment_max"), sem("pad_shifted"), sem("pad_exp")
        s_psum, s_pcomb, s_pmask, s_pqb, s_ptop = (sem(n) for n in (
            "pad_segment_sum", "pad_combined", "pad_masked", "pad_with_q_bias", "pad_top"))
        s_tr = sem("stacks_transposed")
        s_sta, s_std = sem("stacks_ready_by_act"), sem("stacks_ready_by_dve")
        s_s, s_smax = sem("scores_by_query"), sem("row_max")
        s_top, s_nhi, s_nlo = sem("top"), sem("neg_top_hi"), sem("neg_top_lo")
        s_nt, s_nto, s_nd = sem("neg_top_transposed"), sem("neg_top_t_ready"), sem("neg_top_stacked")
        s_avo, s_avt = sem("times_v_copied"), sem("times_v_transposed")
        s_padhalf = sem("pad_sum_of_two")
        s_wsub, s_wexp, s_wmul, s_padsum, s_padout = (sem(n) for n in (
            "pad_weight_arg", "pad_weight_exp", "pad_weight", "pad_sum", "pad_out"))
        s_st, s_ex = sem("scores_by_key"), sem("probs")
        s_av = sem("prob_times_v")
        s_n1, s_n2, s_att = sem("att_sums"), sem("att_reciprocal"), sem("att_normalised")
        s_at, s_ato, s_pr = sem("att_transposed"), sem("att_t_ready"), sem("projection")
        s_xb, s_xa, s_xb2 = sem("x_plus_proj_bias"), sem("x_after_attention"), sem("x_plus_fc2_bias")
        s_f1, s_ge, s_f2, s_xm = sem("fc1"), sem("gelu"), sem("fc2"), sem("x_after_mlp")
        s_out = sem("out_stored")

        def settle(eng, n):
            if not isinstance(n, int):
                eng.nop(nofuse=True)

        def x_slot(n0, n):
            return X[:, bass.ds((n - n0) * TILES, TILES), :] if not isinstance(n, int) \
                else X[:, (n - n0) * TILES:(n - n0 + 1) * TILES, :]

        def run(eng, *steps):
            def iteration(i, items):
                for slot in range(HEADS):
                    for step in steps:
                        for d in items:
                            n, L, par = i(d)
                            step(n, L, par, slot - HEADS * d)

            def static(i):
                items = [d for d in (-2, -1, 0, 1) if 0 <= i + d < 2 * IMAGES]
                iteration(lambda d: (i + d, (i + d) // IMAGES, (i + d) % 2), items)

            for i in range(-1, 3):
                static(i)
            for L in range(2):
                first = IMAGES * L + 3
                with eng.Fori(0, (IMAGES - 4) // 2, 1) as j:
                    for odd in range(2):
                        iteration(lambda d: (j * 2 + (first + odd + d), L, (first + odd + d) % 2), (-2, -1, 0, 1))
                for i in range(first + IMAGES - 4, first + IMAGES if L == 0 else 2 * IMAGES + 2):
                    static(i)

        def peeled(n):
            return isinstance(n, int)

        def from_second(n):
            return not peeled(n) or n >= 2

        def stack_setup(n):
            return STACK_SETUP if peeled(n) and n == 0 else 2 * STACK_SETUP

        block = ctx.enter_context(nc.Block())

        @block.sync
        def _(sp):
            def load_wqkv(L):
                w = layers[L]["qkv_w"]
                sp.dma_start(wqkv_in[:, 0, 0:QKV], w[0:P, :]).then_inc(s_wx, 16)
                sp.dma_start(wqkv_in[0:LO, 1, 0:QKV], w[P:D, :]).then_inc(s_wx, 16)
                sp.dma_start(wqkv_in[LO:P, 1, 0:QKV], w[P:D, :]).then_inc(s_wx, 16)

            def load_w1(L):
                w = layers[L]["fc1_w"]
                sp.dma_start(w1_in[:, 0, :], w[0:P, :]).then_inc(s_wy, 16)
                sp.dma_start(w1_in[0:LO, 1, :], w[P:D, :]).then_inc(s_wy, 16)
                sp.dma_start(w1_in[LO:P, 1, :], w[P:D, :]).then_inc(s_wy, 16)

            sp.dma_start(x_slot(0, 0), x_t[:, 0:TILES, :]).then_inc(s_x0, 16)
            sp.dma_start(ident[:, :], const["ident"]).then_inc(s_id, 16)
            load_wqkv(0)
            for L in range(2):
                sp.dma_start(columns[L][:, :], layers[L]["columns"]).then_inc(s_col[L], 16)
            for name, tile in (("key_rows", key_rows), ("query_mask", query_mask[:, :, :]),
                               ("pad_mask", pad_mask[:, :, :]), ("head_mask", head_mask[:, :])):
                sp.dma_start(tile, const[name]).then_inc(s_const, 16)
            for L in range(2):
                p = layers[L]
                sp.dma_start(qkvb[L][:, :], p["qkv_b"].unsqueeze(0).broadcast_to([P, QKV])).then_inc(s_vec, 16)
                sp.dma_start(rel[L][:, :, :], p["rel"]).then_inc(s_vec, 16)
            sp.dma_start(X[:, TILES:, :], x_t[:, TILES:, :]).then_inc(s_x, 16)
            for L in range(2):
                p = layers[L]
                for tile, name in ((pb[L], "proj_b"), (b2[L], "fc2_b")):
                    sp.dma_start(tile[:, :], p[name].unsqueeze(0).broadcast_to([P, D])).then_inc(s_w, 16)
                sp.dma_start(wp[L][:, 0, :], p["proj_w"][0:P, :]).then_inc(s_w, 16)
                sp.dma_start(wp[L][0:LO, 1, :], p["proj_w"][P:D, :]).then_inc(s_w, 16)
                sp.dma_start(w2[L][:, :, :], p["fc2_w"].rearrange("(m f) n -> f m n", f=P)).then_inc(s_w, 16)
            sp.wait_ge(s_wxl, 1)
            sp.wait_ge(s_wxh, 1)
            load_w1(0)

            def stack_neg_top(n, L, par, t):
                if t == 13:
                    sp.wait_ge(s_nto, n + 1)
                    settle(sp, n)
                    sp.wait_ge(s_s, HEADS * (n + 1))
                    settle(sp, n)
                    for part in range(2):
                        sp.dma_start(q_stack[par][R_MAX + part:R_MAX + part + 1, :, :].bitcast(F32),
                                     neg_top_t[part * HEADS:(part + 1) * HEADS, :].bitcast(F32)).then_inc(s_nd, 16)

            def store(n, L, par, t):
                if t == 12 and peeled(n) and n == 0:
                    sp.wait_ge(s_wyl, 1)
                    sp.wait_ge(s_wyh, 1)
                    load_wqkv(1)
                if t == 0 and peeled(n) and n == IMAGES:
                    sp.wait_ge(s_wxl, 2)
                    sp.wait_ge(s_wxh, 2)
                    load_w1(1)
                if t == 35 and L == 1:
                    sp.wait_ge(s_xm, n + 1)
                    settle(sp, n)
                    dst = out_t[:, bass.ds((n - IMAGES) * TILES, TILES), :] if not peeled(n) \
                        else out_t[:, (n - IMAGES) * TILES:(n - IMAGES + 1) * TILES, :]
                    sp.dma_start(dst, x_slot(IMAGES, n)).then_inc(s_out, 16)

            run(sp, stack_neg_top, store)
            sp.wait_ge(s_out, 16 * IMAGES)

        @block.gpsimd
        def _(pool):
            pool.memset(wqkv_in[:, :, QKV:WCOLS], 0.0).then_inc(s_zero, 1)
            pool.memset(minus_half[:, :], -0.5).then_inc(s_zero, 1)
            for par in range(2):
                pool.memset(v_ones[par][:, :, :, HD:HD + 1], 1.0).then_inc(s_zero, 1)
                pool.memset(v_ones[par][:, :, :, HD + 1:VW], 0.0).then_inc(s_zero, 1)
            pool.memset(q_stack_tok[0][:, :, :, :].bitcast(F32), 0.0).then_inc(s_zero, 1)

            pool.wait_ge(s_zero, ZEROED)

            def constant_rows(par):
                if par == 1:
                    pool.memset(q_stack_tok[1][:, :, :, :].bitcast(F32), 0.0).then_inc(s_zero, 1)
                pool.wait_ge(s_zero, ZEROED + par)
                pool.wait_ge(s_const, C_LOADS)
                for a in range(TILES):
                    pool.tensor_copy(q_stack_tok[par][:, a, :, R_MASK:R_MASK + 4],
                                     query_mask[:, a, :].unsqueeze(1).broadcast_to([P, HEADS, 4])).then_inc(s_stack0, 1)
                pool.tensor_copy(k_stack[par][:, :, :],
                                 key_rows.unsqueeze(1).broadcast_to([P, HEADS, TOK])).then_inc(s_stack0, 1)

            def rstd(i, n):
                pool.wait_ge(n_var[i], n + 1)
                pool.wait_ge(n_hat[i], n)
                settle(pool, n)
                pool.tensor_tensor(norm_rstd[i][:, :], norm_var[i][:, :], minus_half[:, :],
                                   ALU.pow).then_inc(n_rstd[i], 1)

            def add_bias(L, n, bias, done):
                xs = x_slot(IMAGES * L, n)
                pool.tensor_tensor(xs, xs, bias[:, :].unsqueeze(1).broadcast_to([P, TILES, D]),
                                   ALU.add).then_inc(done, 1)

            def split_weights(L):
                pool.wait_ge(s_wx, 48 * (L + 1))
                pool.tensor_scalar(wqkv_in[:, :, D:2 * D], wqkv_in[:, :, D:2 * D], HD ** -0.5, None,
                                   ALU.mult).then_inc(s_wxs, 1)
                pool.memset(wqkv_in[:, :, QKV:WCOLS], 0.0).then_inc(s_wxs, 1)
                pool.wait_ge(s_wxs, L + 2)
                pool.wait_ge(s_qkv, 3 * IMAGES * L)
                pool.tensor_copy(wqkv_hi[:, :, :], wqkv_in[:, :, :]).then_inc(s_wxh, 1)
                pool.wait_ge(s_wxh, L + 1)
                pool.tensor_tensor(wqkv_lo[:, :, :], wqkv_in[:, :, :], wqkv_hi[:, :, :].bitcast(F32),
                                   ALU.subtract).then_inc(s_wxl, 1)

            def split_w1(L):
                pool.wait_ge(s_wy, 48 * (L + 1))
                pool.wait_ge(s_f1, MC * IMAGES * L)
                pool.tensor_copy(w1_hi[:, :, :], w1_in[:, :, :]).then_inc(s_wyh, 1)
                pool.wait_ge(s_wyh, L + 1)
                pool.tensor_tensor(w1_lo[:, :, :], w1_in[:, :, :], w1_hi[:, :, :].bitcast(F32),
                                   ALU.subtract).then_inc(s_wyl, 1)

            def biases_and_pads(n, L, par, t):
                if t in (-11, -9) and peeled(n) and n == 0:
                    constant_rows((t + 11) // 2)
                if t == -12 and peeled(n) and n == IMAGES:
                    split_weights(1)
                if t == 24 and peeled(n) and n == IMAGES:
                    split_w1(1)
                if t == 0:
                    pool.wait_ge(n_hat[0], n + 1)
                    pool.wait_ge(s_w, W_LOADS)
                    settle(pool, n)
                    add_bias(L, n, pb[L], s_xb)
                if t == 5:
                    pool.wait_ge(s_pmax, n + 1)
                    pool.wait_ge(s_psum, n)
                    settle(pool, n)
                    for a in range(TILES):
                        src = rel_tok[:, a, 0:2 * HEADS * WS].rearrange("p (h k) -> p h k", k=WS)
                        dst = pad_e[:, a * 2 * HEADS:(a + 1) * 2 * HEADS, :]
                        for s, (lo, hi) in enumerate(((0, EDGE), (EDGE, WS))):
                            m = seg_max[s][:, a, :, :].rearrange("p w h -> p (w h)").unsqueeze(2)
                            last = pool.tensor_tensor(dst[:, :, lo:hi], src[:, :, lo:hi],
                                                      m.broadcast_to([P, 2 * HEADS, hi - lo]), ALU.subtract)
                    last.then_inc(s_psub, 1)
                if t == 2:
                    pool.wait_ge(s_qkvo, 3 * (n + 1))
                    if from_second(n):
                        pool.wait_ge(s_av, QUADS * (n - 1))
                    settle(pool, n)
                    pool.tensor_copy(v_ones[par][:, :, :, 0:HD],
                                     v_new[:, :, :].rearrange("p a (h c) -> p a h c", c=HD)).then_inc(s_v, 1)
                if t == 9:
                    pool.wait_ge(s_psum, n + 1)
                    pool.wait_ge(s_wsub, n)
                    pool.wait_ge(s_wmul, n)
                    settle(pool, n)
                    for seg, (hs, ws) in enumerate(((0, 1), (1, 1), (1, 0))):
                        pool.tensor_tensor(pad_max[:, seg, :, :], seg_max[hs][:, :, 0, :], seg_max[ws][:, :, 1, :],
                                           ALU.add)
                        last = pool.tensor_tensor(pad_prod[:, seg, :, :], seg_sum[hs][:, :, 0, :],
                                                  seg_sum[ws][:, :, 1, :], ALU.mult)
                    last.then_inc(s_pcomb, 1)
                    pool.wait_ge(s_pcomb, n + 1)
                    settle(pool, n)
                    flat = pad_max[:, :, :, :].rearrange("p s a h -> p s (a h)")
                    pool.tensor_tensor(flat, flat, pad_mask[:, :, :], ALU.add).then_inc(s_pmask, 1)
                    pool.wait_ge(s_pmask, n + 1)
                    settle(pool, n)
                    pool.tensor_tensor(pad_max[:, :, :, :], pad_max[:, :, :, :],
                                       rel_tok[:, :, 2 * HEADS * WS:RW].unsqueeze(1).broadcast_to(
                                           [P, NSEG, TILES, HEADS]), ALU.add).then_inc(s_pqb, 1)
                if t == 13:
                    pool.wait_ge(s_top, n + 1)
                    pool.wait_ge(s_padsum, n)
                    settle(pool, n)
                    pool.tensor_tensor(pad_w[:, :, :], pad_max[:, :, :, :].rearrange("p s a h -> p s (a h)"),
                                       top[:, :, :].rearrange("p a h -> p (a h)").unsqueeze(1).broadcast_to(
                                           [P, NSEG, TILES * HEADS]), ALU.subtract).then_inc(s_wsub, 1)
                if t == 15:
                    pool.wait_ge(s_wexp, n + 1)
                    settle(pool, n)
                    pool.tensor_tensor(pad_w[:, :, :], pad_w[:, :, :],
                                       pad_prod[:, :, :, :].rearrange("p s a h -> p s (a h)"),
                                       ALU.mult).then_inc(s_wmul, 1)
                if t == 17:
                    pool.wait_ge(s_wmul, n + 1)
                    pool.wait_ge(s_n1, n)
                    pool.wait_ge(s_padout, n)
                    settle(pool, n)
                    sums = pad_sum[:, :, :].rearrange("p a h -> p (a h)")
                    pool.tensor_tensor(sums, pad_w[:, 0, :], pad_w[:, 1, :], ALU.add).then_inc(s_padhalf, 1)
                    pool.wait_ge(s_padhalf, n + 1)
                    settle(pool, n)
                    pool.tensor_tensor(sums, sums, pad_w[:, 2, :], ALU.add).then_inc(s_padsum, 1)
                if t == 18:
                    pool.wait_ge(s_padsum, n + 1)
                    pool.wait_ge(s_n1, n)
                    settle(pool, n)
                    for a in range(TILES):
                        last = pool.tensor_tensor(
                            pad_out[:, a, :, :],
                            qkvb[L][:, 2 * D:QKV].rearrange("p (h c) -> p h c", c=HD),
                            pad_sum[:, a, :].unsqueeze(2).broadcast_to([P, HEADS, HD]), ALU.mult)
                    last.then_inc(s_padout, 1)
                if t == 31:
                    pool.wait_ge(n_hat[1], n + 1)
                    settle(pool, n)
                    add_bias(L, n, b2[L], s_xb2)

            def roots(n, L, par, t):
                if t == -12:
                    rstd(0, n)
                if t == 29:
                    rstd(1, n)

            run(pool, biases_and_pads, roots)

        @block.scalar
        def _(act):
            act.wait_ge(s_wxs, 1)
            act.wait_ge(s_zero, ZEROED)
            act.activation(wqkv_hi[:, :, :], wqkv_in[:, :, :], ACT.Copy).then_inc(s_wxh, 1)

            def affine(i, n, L, bank):
                act.wait_ge(n_tr[i], n + 1)
                act.wait_ge(n_hi[i], n)
                act.wait_ge(n_lo[i], n)
                act.wait_ge(s_col[L], 16)
                norm = (n1, n2)[i][L]
                for c in range(2):
                    last = act.activation(xn[i][:, c, :], bank[:, c * TOK:(c + 1) * TOK], ACT.Identity,
                                          bias=norm[:, c, 1:2], scale=norm[:, c, 0:1])
                last.then_inc(n_aff[i], 1)

            def exps(n, L, par, t):
                h = t - 15
                if 0 <= h < HEADS:
                    act.wait_ge(s_st, HEADS * n + h + 1)
                    if not (peeled(n) and n == 0) or h >= NP:
                        act.wait_ge(s_av, QUADS * n + (h - NP) // QUAD + 1)
                    act.activation(probs[h % NP][:, :, :], KB[h % 2][:, :].rearrange("p (k t) -> p k t", k=2),
                                   ACT.Exp).then_inc(s_ex, 1)

            def chain(n, L, par, t):
                if t == -5:
                    act.wait_ge(s_qt, n + 1)
                    act.wait_ge(s_rel, 2 * n)
                    act.wait_ge(s_rt, TILES * n)
                    act.activation(q_t[:, :, :], FB[0:GF, :].rearrange("p (g t) -> p g t", g=2),
                                   ACT.Copy).then_inc(s_qto, 1)
                if t == -4:
                    act.wait_ge(s_rel, 2 * n + 1)
                    act.wait_ge(s_rt, TILES * n)
                    act.activation(rel_t[:, 0, :, :], FB[0:GR, :].rearrange("p (g t) -> p g t", g=2),
                                   ACT.Copy).then_inc(s_relo, 1)
                if t == -1:
                    act.wait_ge(s_pqb, n)
                    act.wait_ge(s_rlo, TILES * n)
                    act.wait_ge(s_psub, n)
                    act.wait_ge(s_rt, TILES * (n + 1))
                    act.activation(rel_tok[:, 1, 0:4 * GR].rearrange("p (x h k) -> p x h k", h=GH, k=WS),
                                   FB[:, 0:4 * GR].rearrange("p (x k h) -> p x h k", h=GH, k=WS), ACT.Copy)
                    act.activation(rel_tok[:, 1, 4 * GR:RW], FB[:, 4 * GR:RW], ACT.Copy).then_inc(s_rto, 1)
                if t == 6:
                    act.wait_ge(s_psub, n + 1)
                    act.activation(pad_e[:, :, :], pad_e[:, :, :], ACT.Exp).then_inc(s_pexp, 1)
                if t == 14:
                    act.wait_ge(s_wsub, n + 1)
                    act.activation(pad_w[:, :, :], pad_w[:, :, :], ACT.Exp).then_inc(s_wexp, 1)
                if t == 3 and peeled(n) and n == 0:
                    act.wait_ge(s_wy, 48)
                    act.activation(w1_hi[:, :, :], w1_in[:, :, :], ACT.Copy).then_inc(s_wyh, 1)
                if t == 28:
                    act.wait_ge(s_at, n + 1)
                    act.wait_ge(s_pr, n)
                    act.activation(att_t[:, 0, :], BB[0][:, 0:TOK], ACT.Copy)
                    act.activation(att_t[0:LO, 1, :], BB[0][0:LO, TOK:2 * TOK], ACT.Copy).then_inc(s_ato, 1)

            def stacks(n, L, par, t):
                if 0 <= t < HEADS and not STACK_ON_DVE[t]:
                    h = t
                    act.wait_ge(s_tr, HEADS * n + h + 1)
                    act.wait_ge(s_stack0, stack_setup(n))
                    if from_second(n):
                        act.wait_ge(s_st, HEADS * (n - 2) + h + 1)
                    act.activation(q_stack[par][:, h, :], TB[:, 0:TOK], ACT.Copy)
                    act.activation(k_stack[par][0:KROWS, h, :], TB[0:KROWS, TOK:2 * TOK],
                                   ACT.Copy).then_inc(s_sta, 1)

            def neg_top_out(n, L, par, t):
                if t == 13:
                    act.wait_ge(s_nt, n + 1)
                    act.wait_ge(s_nd, 32 * n)
                    act.activation(neg_top_t[:, :], BB[1][0:2 * HEADS, 0:TOK], ACT.Copy).then_inc(s_nto, 1)

            def chain_end(n, L, par, t):
                if t == -10:
                    affine(0, n, L, FB)
                if t == 30:
                    affine(1, n, L, BB[0])

            def gelus(n, L, par, t):
                if t == 32:
                    for m in range(MC):
                        act.wait_ge(s_f1, MC * n + 2 * (m // 2) + 2)
                        act.wait_ge(s_f2, TILES * n)
                        act.activation(hid[:, m, :], fc1_psum(m), ACT.Gelu,
                                       bias=b1[L][:, m:m + 1]).then_inc(s_ge, 1)

            run(act, chain, exps, stacks, neg_top_out, chain_end, gelus)

        @block.vector
        def _(dve):
            def scale_k_weights():
                dve.wait_ge(s_wx, 48)
                dve.tensor_scalar(wqkv_in[:, :, D:2 * D], wqkv_in[:, :, D:2 * D], HD ** -0.5, None,
                                  ALU.mult).then_inc(s_wxs, 1)

            def setup_vectors():
                dve.wait_ge(s_vec, V_LOADS)
                for l in range(2):
                    dve.wait_ge(s_col[l], 16)
                dve.wait_ge(s_const, C_LOADS)
                for l in range(2):
                    dve.tensor_scalar(qkvb[l][:, D:2 * D], qkvb[l][:, D:2 * D], HD ** -0.5, None,
                                      ALU.mult).then_inc(s_setup, 1)
                    dve.tensor_scalar(kb[l], kb[l], HD ** -0.5, None, ALU.mult).then_inc(s_kb, 1)
                    dve.wait_ge(s_kb, l + 1)
                    dve.tensor_tensor(kb_blocks[l][:, :, :],
                                      head_mask[:, :].unsqueeze(1).broadcast_to([GF, 2, GH]),
                                      kb[l].unsqueeze(2).broadcast_to([GF, 2, GH]),
                                      ALU.mult).then_inc(s_setup, 1)
                    offsets = 2 * (2 * WS - 1)
                    dve.tensor_tensor(
                        rel_heads[l][:, :, :, :].rearrange("p w o h -> p (w o) h"),
                        rel[l][:, :, :].rearrange("p w o -> p (w o)").unsqueeze(2).broadcast_to([GF, offsets, GH]),
                        head_mask[:, :].unsqueeze(1).broadcast_to([GF, offsets, GH]), ALU.mult).then_inc(s_setup, 1)

            def norm_stats(i, n, L):
                xs = x_slot(IMAGES * L, n)
                dve.wait_ge(n_aggr[i], n)
                settle(dve, n)
                for a in range(TILES):
                    last = dve.bn_stats(norm_s[i][:, a, :], xs[:, a, :])
                last.then_inc(n_stat[i], 1)
                dve.wait_ge(n_stat[i], n + 1)
                dve.wait_ge(n_hat[i], n)
                settle(dve, n)
                for a in range(TILES):
                    last = dve.bn_aggr(norm_mv[i][:, a, :], norm_s[i][:, a, :])
                last.then_inc(n_aggr[i], 1)
                dve.wait_ge(n_aggr[i], n + 1)
                dve.wait_ge(n_rstd[i], n)
                dve.tensor_scalar(norm_var[i][:, :], norm_mv[i][:, :, 1], EPS[L], None, ALU.add).then_inc(n_var[i], 1)

            def norm_hat(i, n, L):
                xs = x_slot(IMAGES * L, n)
                dve.wait_ge(n_rstd[i], n + 1)
                dve.wait_ge(n_tr[i], n)
                for a in range(TILES):
                    mean, r = norm_mv[i][:, a, 0:1], norm_rstd[i][:, a:a + 1]
                    dve.tensor_scalar(xhat[i][:, a, 0:P], xs[:, a, 0:P], mean, r, ALU.subtract, ALU.mult)
                    last = dve.tensor_scalar(
                        xhat[i][:, a, P:2 * P].rearrange("p (t f) -> p t f", t=2),
                        xs[:, a, P:D].unsqueeze(1).broadcast_to([P, 2, LO]), mean, r, ALU.subtract, ALU.mult)
                last.then_inc(n_hat[i], 1)

            def split_norm(i, n):
                dve.wait_ge(n_aff[i], n + 1)
                dve.wait_ge(s_qkv if i == 0 else s_f1, (3 if i == 0 else MC) * n)
                dve.tensor_copy(xn_hi[i][:, :, :], xn[i][:, :, :]).then_inc(n_hi[i], 1)
                dve.wait_ge(n_hi[i], n + 1)
                dve.tensor_tensor(xn_lo[i][:, :], xn[i][:, 0, :], xn_hi[i][:, 0, :].bitcast(F32), ALU.subtract)
                dve.tensor_tensor(xn_hi[i][LO:P, 1, :], xn[i][LO:P, 1, :], xn_hi[i][LO:P, 1, :].bitcast(F32),
                                  ALU.subtract).then_inc(n_lo[i], 1)

            def split_rel(n, par, a):
                dve.wait_ge(s_rto, TILES * n + a + 1)
                rows = q_stack_tok[par][:, a, :, R_RHI:R_RLO].rearrange("p h (w k) -> p w h k", w=2)
                low = q_stack_tok[par][:, a, :, R_RLO:R_MASK].rearrange("p h (w k) -> p w h k", w=2)
                src = rel_tok[:, a, 0:2 * HEADS * WS].rearrange("p (w h k) -> p w h k", w=2, k=WS)
                dve.tensor_copy(rows, src).then_inc(s_rhi, 1)
                dve.wait_ge(s_rhi, TILES * n + a + 1)
                dve.tensor_tensor(low, src, rows.bitcast(F32), ALU.subtract).then_inc(s_rlo, 1)

            def front_out(n, L, par, t):
                if t in (-8, -7):
                    a = t + 8
                    dve.wait_ge(s_qkv, 3 * n + a + 1)
                    dve.wait_ge(s_setup, SETUP_DVE)
                    if a == 0:
                        dve.wait_ge(s_qkh, n)
                        dve.wait_ge(s_qkl, n)
                        dve.wait_ge(s_qt, n)
                    dve.tensor_tensor(qk[:, a, :], FB[:, 0:2 * D], qkvb[L][:, 0:2 * D], ALU.add).then_inc(s_qkvo, 1)
                if t == -6:
                    dve.wait_ge(s_qkv, 3 * (n + 1))
                    dve.wait_ge(s_v, n)
                    dve.tensor_tensor(v_new[:, :, :],
                                      FB[:, :].rearrange("p (a f) -> p a f", a=TILES)[:, :, 0:D],
                                      qkvb[L][:, 2 * D:QKV].unsqueeze(1).broadcast_to([P, TILES, D]),
                                      ALU.add).then_inc(s_qkvo, 1)
                if t == -2:
                    dve.wait_ge(s_pqb, n)
                    dve.wait_ge(s_rlo, TILES * n)
                    dve.wait_ge(s_psub, n)
                    dve.wait_ge(s_rt, TILES * n + 1)
                    dve.tensor_copy(rel_tok[:, 0, 0:4 * GR].rearrange("p (x h k) -> p x h k", h=GH, k=WS),
                                    FB[:, 0:4 * GR].rearrange("p (x k h) -> p x h k", h=GH, k=WS))
                    dve.tensor_copy(rel_tok[:, 0, 4 * GR:RW], FB[:, 4 * GR:RW]).then_inc(s_rto, 1)
                if t == -3:
                    dve.wait_ge(s_rel, 2 * (n + 1))
                    dve.wait_ge(s_rt, TILES * n)
                    dve.tensor_copy(rel_t[:, 1, :, :].rearrange("p g (r c) -> p g r c", c=SIDE),
                                    FB[0:GR, :].rearrange("p (g c r) -> p g r c", g=2, r=SIDE)).then_inc(s_relo, 1)

            def chain(n, L, par, t):
                if t == -11 and peeled(n) and n == 0:
                    scale_k_weights()
                if t == -6:
                    dve.wait_ge(s_qkvo, 3 * (n + 1))
                    dve.wait_ge(s_stack0, stack_setup(n))
                    if from_second(n):
                        dve.wait_ge(s_tr, HEADS * (n - 1))
                    for a in range(TILES):
                        dve.tensor_copy(
                            q_stack_tok[par][:, a, :, 0:2 * HD].rearrange("p h (t c) -> p h t c", t=2),
                            qk[:, a, 0:D].rearrange("p (h c) -> p h c", c=HD).unsqueeze(2)
                            .broadcast_to([P, HEADS, 2, HD]))
                    k_in = qk[:, :, D:2 * D].rearrange("p a (h c) -> p a h c", c=HD)
                    for at in (0, 2 * HD):
                        last = dve.tensor_copy(k_stack_tok[par][:, :, :, at:at + HD], k_in)
                    last.then_inc(s_qkh, 1)
                if t == -4:
                    dve.wait_ge(s_qkh, n + 1)
                    dve.tensor_tensor(
                        q_stack_tok[par][:, :, :, R_QLO:R_QLO + HD],
                        qk[:, :, 0:D].rearrange("p a (h c) -> p a h c", c=HD),
                        q_stack_tok[par][:, :, :, 0:HD].bitcast(F32), ALU.subtract)
                    dve.tensor_tensor(
                        k_stack_tok[par][:, :, :, HD:2 * HD],
                        qk[:, :, D:2 * D].rearrange("p a (h c) -> p a h c", c=HD),
                        k_stack_tok[par][:, :, :, 0:HD].bitcast(F32), ALU.subtract).then_inc(s_qkl, 1)
                if t == 4:
                    dve.wait_ge(s_rto, TILES * (n + 1))
                    dve.wait_ge(s_psub, n)
                    dve.wait_ge(s_pcomb, n)
                    rows = rel_tok[:, :, 0:2 * HEADS * WS].rearrange("p a (h k) -> p a h k", k=WS)
                    for s, (lo, hi) in enumerate(((0, EDGE), (EDGE, WS))):
                        last = dve.tensor_reduce(seg_max[s][:, :, :, :].rearrange("p a w h -> p a (w h)"),
                                                 rows[:, :, :, lo:hi], AX, ALU.max)
                    last.then_inc(s_pmax, 1)
                if t == 8:
                    dve.wait_ge(s_pexp, n + 1)
                    dve.wait_ge(s_pcomb, n)
                    for s, (lo, hi) in enumerate(((0, EDGE), (EDGE, WS))):
                        last = dve.tensor_reduce(
                            seg_sum[s][:, :, :, :].rearrange("p a w h -> p (a w h)"), pad_e[:, :, lo:hi], AX, ALU.add)
                    last.then_inc(s_psum, 1)
                if t == 10:
                    dve.wait_ge(s_pqb, n + 1)
                    dve.wait_ge(s_top, n)
                    dve.tensor_reduce(pad_top[:, :], pad_max[:, :, :, :].rearrange("p s a h -> p (a h) s"), AX,
                                      ALU.max).then_inc(s_ptop, 1)
                if t == 31:
                    split_norm(1, n)
                if t == 27:
                    dve.wait_ge(s_avt, n + 1)
                    dve.wait_ge(s_padout, n + 1)
                    dve.wait_ge(s_padsum, n + 1)
                    dve.wait_ge(s_at, n)
                    dve.wait_ge(s_att, n)
                    a4 = att[:, :, :].rearrange("p a (h c) -> p a h c", c=HD)
                    for lo, hi in ((0, 2 * QUAD), (2 * QUAD, HEADS)):
                        o = attention_psum(slice(None), lo, hi)
                        dve.tensor_tensor(a4[:, :, lo:hi, :], o[:, :, :, 0:HD], pad_out[:, :, lo:hi, :], ALU.add)
                        last = dve.tensor_tensor(den[:, :, lo:hi], o[:, :, :, HD], pad_sum[:, :, lo:hi], ALU.add)
                    last.then_inc(s_n1, 1)
                    dve.wait_ge(s_n1, n + 1)
                    dve.reciprocal(den[:, :, :], den[:, :, :]).then_inc(s_n2, 1)
                    dve.wait_ge(s_n2, n + 1)
                    dve.tensor_tensor(a4, a4, den[:, :, :].unsqueeze(3).broadcast_to([P, TILES, HEADS, HD]),
                                      ALU.mult).then_inc(s_att, 1)
                if t == 29:
                    dve.wait_ge(s_xa, n + 1)
                    norm_stats(1, n, L)
            def row_maxima(n, L, par, t):
                if 0 <= t < HEADS and STACK_ON_DVE[t]:
                    dve.wait_ge(s_tr, HEADS * n + t + 1)
                    dve.wait_ge(s_stack0, stack_setup(n))
                    if from_second(n):
                        dve.wait_ge(s_st, HEADS * (n - 2) + t + 1)
                    dve.tensor_copy(q_stack[par][:, t, :], TB[:, 0:TOK])
                    dve.tensor_copy(k_stack[par][0:KROWS, t, :], TB[0:KROWS, TOK:2 * TOK]).then_inc(s_std, 1)
                h = t - 1
                if 0 <= h < HEADS:
                    dve.wait_ge(s_s, HEADS * n + h + 1)
                    if h == 0:
                        dve.wait_ge(s_top, n)
                    dve.tensor_reduce(row_max[:, h, :], QB[:, :].rearrange("p (a t) -> p a t", a=TILES), AX,
                                      ALU.max).then_inc(s_smax, 1)

            def after_maxima(n, L, par, t):
                if t in (18, 22, 26):
                    g = (t - 18) // QUAD
                    dve.wait_ge(s_av, QUADS * n + g + 1)
                    dve.wait_ge(s_avt, n)
                    dve.tensor_copy(av_t[:, g, :], VB[:, 0:TOK]).then_inc(s_avo, 1)

            def chain_end(n, L, par, t):
                if t == -10:
                    split_norm(0, n)
                    if peeled(n) and n == 0:
                        dve.wait_ge(s_wxh, 1)
                        dve.tensor_tensor(wqkv_lo[:, :, :], wqkv_in[:, :, :], wqkv_hi[:, :, :].bitcast(F32),
                                          ALU.subtract).then_inc(s_wxl, 1)
                        setup_vectors()
                if t in (-2, -1):
                    split_rel(n, par, t + 2)
                if t == -11:
                    norm_hat(0, n, L)
                if t == 29:
                    norm_hat(1, n, L)
                if t == 12:
                    dve.wait_ge(s_smax, HEADS * (n + 1))
                    dve.wait_ge(s_ptop, n + 1)
                    dve.wait_ge(s_nlo, n)
                    dve.wait_ge(s_wsub, n)
                    dve.tensor_tensor(top[:, :, :], row_max[:, :, :].rearrange("p h a -> p a h"),
                                      pad_top[:, :].rearrange("p (a h) -> p a h", a=TILES), ALU.max).then_inc(s_top, 1)
                    dve.wait_ge(s_top, n + 1)
                    dve.wait_ge(s_nt, n)
                    dve.tensor_scalar(neg_top[:, :, 0, :], top[:, :, :], -1.0, None, ALU.mult).then_inc(s_nhi, 1)
                    dve.wait_ge(s_nhi, n + 1)
                    dve.scalar_tensor_tensor(neg_top[:, :, 1, :], top[:, :, :], -1.0, neg_top[:, :, 0, :].bitcast(F32),
                                             ALU.mult, ALU.subtract).then_inc(s_nlo, 1)
                if t == 4 and peeled(n) and n == 0:
                    dve.wait_ge(s_wyh, 1)
                    dve.tensor_tensor(w1_lo[:, :, :], w1_in[:, :, :], w1_hi[:, :, :].bitcast(F32),
                                      ALU.subtract).then_inc(s_wyl, 1)

            def finish(n, L, par, t):
                if t == -12:
                    if peeled(n) and n == 0:
                        dve.wait_ge(s_x0, 16)
                    else:
                        dve.wait_ge(s_x, 16)
                    if L == 1:
                        dve.wait_ge(s_xm, n - IMAGES + 1)
                    norm_stats(0, n, L)
                if t == 28:
                    xs = x_slot(IMAGES * L, n)
                    dve.wait_ge(s_pr, n + 1)
                    dve.wait_ge(s_xb, n + 1)
                    dve.tensor_tensor(xs, xs, BB[1][:, 0:TILES * D].rearrange("p (a d) -> p a d", d=D),
                                      ALU.add).then_inc(s_xa, 1)
                if t == 35:
                    xs = x_slot(IMAGES * L, n)
                    dve.wait_ge(s_f2, TILES * (n + 1))
                    dve.wait_ge(s_xb2, n + 1)
                    dve.tensor_tensor(xs, xs, BB[0][:, 0:TILES * D].rearrange("p (a d) -> p a d", d=D),
                                      ALU.add).then_inc(s_xm, 1)

            run(dve, front_out, chain, row_maxima, after_maxima, chain_end, finish)

        @block.tensor
        def _(pe):
            def split_product(psum, chunks):
                for i, (lhs, rhs) in enumerate(chunks):
                    last = pe.matmul(psum, lhs, rhs, start=(i == 0), stop=(i == len(chunks) - 1))
                return last

            def norm_transposes(i, n, bank):
                pe.wait_ge(n_hat[i], n + 1)
                for c in range(2):
                    for a in range(TILES):
                        last = pe.transpose(bank[:, c * TOK + a * P:c * TOK + (a + 1) * P],
                                            xhat[i][:, a, c * P:(c + 1) * P], ident[:, :])
                last.then_inc(n_tr[i], 1)

            def xn_times(psum, a, cols):
                tok = slice(a * P, (a + 1) * P)
                return split_product(psum, [
                    (xn_hi[0][:, 0, tok], wqkv_hi[:, 0, cols]), (xn_hi[0][:, 0, tok], wqkv_lo[:, 0, cols]),
                    (xn_lo[0][:, tok], wqkv_hi[:, 0, cols]),
                    (xn_hi[0][:, 1, tok], wqkv_hi[:, 1, cols]), (xn_hi[0][:, 1, tok], wqkv_lo[:, 1, cols])])

            def front(n, L, par, t):
                if t in (-9, -8):
                    a = t + 9
                    if a == 0:
                        pe.wait_ge(n_lo[0], n + 1)
                        pe.wait_ge(s_wxl, L + 1)
                        pe.wait_ge(n_aff[0], n + 1)
                    else:
                        pe.wait_ge(s_qkvo, 3 * n + 1)
                    xn_times(FB[:, 0:2 * D], a, slice(0, 2 * D)).then_inc(s_qkv, 1)
                if t == -7:
                    pe.wait_ge(s_qkvo, 3 * n + 2)
                    for a in range(TILES):
                        last = xn_times(FB[:, a * TOK:(a + 1) * TOK], a, slice(2 * D, WCOLS))
                    last.then_inc(s_qkv, 1)
                if t == -6:
                    pe.wait_ge(s_qkvo, 3 * (n + 1))
                    for g in range(2):
                        for a in range(TILES):
                            last = pe.transpose(FB[0:GF, g * TOK + a * P:g * TOK + (a + 1) * P],
                                                qk[:, a, g * GF:(g + 1) * GF], ident[:, :])
                    last.then_inc(s_qt, 1)
                if t in (-5, -4):
                    w = t + 5
                    if w == 0:
                        pe.wait_ge(s_qto, n + 1)
                        pe.wait_ge(s_setup, SETUP_DVE)
                    else:
                        pe.wait_ge(s_relo, 2 * n + 1)
                    grid = q_t[:, :, :].rearrange("p g (r c) -> p g r c" if w == 0 else "p g (r c) -> p g c r", c=SIDE)
                    dst = FB[0:GR, :].rearrange("p (g r c) -> p g r c", g=2, c=SIDE)
                    for i in range(WS):
                        at = slice(i, i + WS + 1, WS) if i < EDGE else slice(i, i + 1)
                        last = pe.matmul(dst[:, :, at, :], rel_heads[L][:, w, WS - 1 - i:2 * WS - 1 - i, :]
                                         .rearrange("p k h -> p (k h)"), grid[:, :, at, :], start=True, stop=True)
                    last.then_inc(s_rel, 1)
                if t in (-3, -2):
                    a = t + 3
                    if a == 0:
                        pe.wait_ge(s_relo, 2 * (n + 1))
                    else:
                        pe.wait_ge(s_rto, TILES * n + 1)
                    for w in range(2):
                        for g in range(2):
                            col = (w * 2 + g) * GR
                            pe.transpose(FB[:, col:col + GR], rel_t[:, w, g, a * P:(a + 1) * P],
                                         ident[0:GR, 0:GR])
                    for g in range(2):
                        col = 4 * GR + g * GH
                        last = pe.matmul(FB[:, col:col + GH], q_t[:, g, a * P:(a + 1) * P],
                                         kb_blocks[L][:, g, :], start=True, stop=True)
                    last.then_inc(s_rt, 1)

            def scores_by_key(n, L, par, t):
                h = t - 14
                if 0 <= h < HEADS:
                    if h == 0:
                        pe.wait_ge(s_nd, 32 * (n + 1))
                    if not (peeled(n) and n == 0) or h >= 2:
                        pe.wait_ge(s_ex, HEADS * n + h - 1)
                    for c in range(2):
                        last = pe.matmul(KB[h % 2][:, c * TOK:(c + 1) * TOK], k_stack[par][:, h, c * P:(c + 1) * P],
                                         q_stack[par][:, h, :], start=True, stop=True)
                    last.then_inc(s_st, 1)

            def times_v(n, L, par, t):
                if t in (18, 22, 26):
                    g = (t - 18) // QUAD
                    pe.wait_ge(s_ex, HEADS * n + (g + 1) * QUAD)
                    if g == 0:
                        pe.wait_ge(s_v, n + 1)
                        pe.wait_ge(s_n1, n)
                    if not (peeled(n) and n == 0 and g == 0):
                        pe.wait_ge(s_avo, QUADS * n + g)
                    for c in range(2):
                        for i in range(QUAD):
                            h = g * QUAD + i
                            last = pe.matmul(VB[i * VW:(i + 1) * VW, 0:TOK], v_ones[par][:, c, h, :],
                                             probs[h % NP][:, c, :], start=(c == 0), stop=(c == 1))
                    last.then_inc(s_av, 1)

            def evacuated(n, h):
                by_dve = sum(STACK_ON_DVE[:h + 1])
                if STACK_ON_DVE[h]:
                    pe.wait_ge(s_std, sum(STACK_ON_DVE) * n + by_dve)
                else:
                    pe.wait_ge(s_sta, (HEADS - sum(STACK_ON_DVE)) * n + h + 1 - by_dve)

            def stacks(n, L, par, t):
                h = t - 1
                if 0 <= h < HEADS:
                    evacuated(n, h)
                    if not (peeled(n) and n == 0 and h == 0):
                        pe.wait_ge(s_smax, HEADS * n + h)
                    for a in range(TILES):
                        last = pe.matmul(QB[:, a * TOK:(a + 1) * TOK], q_stack[par][:, h, a * P:(a + 1) * P],
                                         k_stack[par][:, h, :], start=True, stop=True)
                    last.then_inc(s_s, 1)

            def transposes(n, L, par, t):
                h = t
                if 0 <= h < HEADS:
                    if h == 0:
                        pe.wait_ge(s_qkl, n + 1)
                        pe.wait_ge(s_qkh, n + 1)
                        pe.wait_ge(s_rlo, TILES * (n + 1))
                        pe.wait_ge(s_rhi, TILES * (n + 1))
                        pe.wait_ge(s_stack0, stack_setup(n))
                        if from_second(n):
                            evacuated(n - 1, HEADS - 1)
                        elif n == 1:
                            evacuated(0, HEADS - 1)
                    else:
                        evacuated(n, h - 1)
                    for a in range(TILES):
                        pe.transpose(TB[:, a * P:(a + 1) * P], q_stack_tok[par][:, a, h, :].bitcast(F32), ident[:, :])
                    settle(pe, n)
                    for a in range(TILES):
                        last = pe.transpose(TB[0:KROWS, TOK + a * P:TOK + (a + 1) * P],
                                            k_stack_tok[par][:, a, h, :].bitcast(F32), ident[:, :])
                    last.then_inc(s_tr, 1)

            def fc1(n, L, m):
                f = slice(m * P, (m + 1) * P)
                split_product(fc1_psum(m), [
                    (w1_hi[:, 0, f], xn_hi[1][:, 0, :]), (w1_lo[:, 0, f], xn_hi[1][:, 0, :]),
                    (w1_hi[:, 0, f], xn_lo[1][:, :]),
                    (w1_hi[:, 1, f], xn_hi[1][:, 1, :]), (w1_lo[:, 1, f], xn_hi[1][:, 1, :])]).then_inc(s_f1, 1)

            def fc1_pair(n, L, pair):
                if pair == 0:
                    pe.wait_ge(n_lo[1], n + 1)
                    pe.wait_ge(s_wyl, L + 1)
                    pe.wait_ge(s_xa, n + 1)
                elif pair == 1:
                    pe.wait_ge(n_aff[1], n + 1)
                else:
                    pe.wait_ge(s_ge, MC * n + 2)
                for m in (2 * pair, 2 * pair + 1):
                    fc1(n, L, m)

            def middle(n, L, par, t):
                if t == 13:
                    pe.wait_ge(s_nlo, n + 1)
                    pe.wait_ge(s_nhi, n + 1)
                    if from_second(n):
                        pe.wait_ge(s_ge, MC * (n - 1))
                    for a in range(TILES):
                        last = pe.transpose(BB[1][0:2 * HEADS, a * P:(a + 1) * P],
                                            neg_top[:, a, :, :].rearrange("p t h -> p (t h)").bitcast(F32), ident[:, :])
                    last.then_inc(s_nt, 1)
                if t == 30:
                    pe.wait_ge(s_ato, n + 1)
                    norm_transposes(1, n, BB[0])
                if t == -10:
                    pe.wait_ge(s_rto, TILES * n)
                    pe.wait_ge(s_id, 16)
                    norm_transposes(0, n, FB)
                if t == 28:
                    pe.wait_ge(s_ato, n + 1)
                    pe.wait_ge(s_w, W_LOADS)
                    pe.wait_ge(s_nto, min(n + 2, 2 * IMAGES) if peeled(n) else n + 2)
                    for a in range(TILES):
                        last = split_product(BB[1][:, a * D:(a + 1) * D], [
                            (att_t[:, 0, a * P:(a + 1) * P], wp[L][:, 0, :]),
                            (att_t[0:LO, 1, a * P:(a + 1) * P], wp[L][0:LO, 1, :])])
                    last.then_inc(s_pr, 1)
                if t == 33:
                    fc1_pair(n, L, 2)

            def to_tokens(n, L, par, t):
                if t == 26:
                    pe.wait_ge(s_avo, QUADS * (n + 1))
                    pe.wait_ge(s_xm, n)
                    for g in range(QUADS):
                        for a in range(TILES):
                            last = pe.transpose(attention_psum(a, g * QUAD, (g + 1) * QUAD),
                                                av_t[:, g, a * P:(a + 1) * P], ident[:, :])
                    last.then_inc(s_avt, 1)

            def back(n, L, par, t):
                if t == 27:
                    pe.wait_ge(s_att, n + 1)
                    pe.wait_ge(s_xm, n)
                    for a in range(TILES):
                        pe.transpose(BB[0][:, a * P:(a + 1) * P], att[:, a, 0:P], ident[:, :])
                        last = pe.transpose(BB[0][0:LO, TOK + a * P:TOK + (a + 1) * P], att[:, a, P:D], ident[:, :])
                    last.then_inc(s_at, 1)
                if t in (31, 32):
                    fc1_pair(n, L, t - 31)
                if t in (34, 35):
                    a = t - 34
                    for m in range(MC):
                        if a == 0:
                            pe.wait_ge(s_ge, MC * n + max(m + 1, 4))
                        last = pe.matmul(BB[0][:, a * D:(a + 1) * D], hid[:, m, a * P:(a + 1) * P], w2[L][:, m, :],
                                         start=(m == 0), stop=(m == MC - 1))
                    last.then_inc(s_f2, 1)

            run(pe, stacks, transposes, middle, front, back, times_v, scores_by_key, to_tokens)


def kernel(**inputs):
    import numpy as np
    import concourse.bacc as bacc
    from concourse.bass_utils import run_bass_kernel_spmd

    nc = bacc.Bacc("TRN2", target_bir_lowering=False, num_devices=1)
    arrays = {}

    def dram(name, a):
        a = np.ascontiguousarray(a)
        arrays[name] = a
        return nc.dram_tensor(name, a.shape, mybir.dt.from_np(a.dtype), kind="ExternalInput").ap()

    names = [dict(qkv_w="L0_conv_qkv_w", qkv_b="L0_conv_qkv_b", proj_w="L0_conv_proj_w", proj_b="L0_conv_proj_b",
                  rel_h="L0_conv_rel_pos_h", rel_w="L0_conv_rel_pos_w", n1_w="L0_conv_norm1_w",
                  n1_b="L0_conv_norm1_b", n2_w="L0_conv_norm2_w", n2_b="L0_conv_norm2_b", fc1_w="L0_conv_fc1_w",
                  fc1_b="L0_conv_fc1_b", fc2_w="L0_conv_fc2_w", fc2_b="L0_conv_fc2_b"),
             dict(qkv_w="L1_conv_w_qkv", qkv_b="L1_conv_b_qkv", proj_w="L1_conv_w_proj", proj_b="L1_conv_b_proj",
                  rel_h="L1_conv_rel_pos_h", rel_w="L1_conv_rel_pos_w", n1_w="L1_conv_ln1_g", n1_b="L1_conv_ln1_b",
                  n2_w="L1_conv_ln2_g", n2_b="L1_conv_ln2_b", fc1_w="L1_conv_w_fc1", fc1_b="L1_conv_b_fc1",
                  fc2_w="L1_conv_w_fc2", fc2_b="L1_conv_b_fc2")]
    x = dram("in_x", inputs["x"])
    layers = []
    for L, of in enumerate(names):
        layer = {k: dram(f"in_{k}_{L}", inputs[of[k]]) for k in LAYER_IN}
        columns = np.zeros((P, COLS), np.float32)
        for at, name in enumerate(("n1_w", "n1_b", "n2_w", "n2_b")):
            v, at = np.asarray(inputs[of[name]]), at + 2 * (at // 2)
            columns[:, at] = v[:P]
            columns[:, at + 2] = np.tile(v[P:], 2)
        columns[:, 8:8 + MC] = np.asarray(inputs[of["fc1_b"]]).reshape(MC, P).T
        columns[:GF, 8 + MC:] = np.asarray(inputs[of["qkv_b"]])[D:2 * D].reshape(2, GF).T
        layer["columns"] = dram(f"in_columns_{L}", columns)
        rels = [np.tile(np.asarray(inputs[of[r]])[::-1].T, (GH, 1)) for r in ("rel_h", "rel_w")]
        layer["rel"] = dram(f"in_rel_{L}", np.stack(rels, axis=1))
        layers.append(layer)

    r, c = np.divmod(np.arange(TOK), SIDE)
    window = 2 * (r >= WS) + (c >= WS)
    rows = np.zeros((P, TOK), np.float32)
    t = np.arange(TOK)
    for at in (R_RHI, R_RLO):
        rows[at + r % WS, t] = 1
        rows[at + WS + c % WS, t] = 1
    rows[R_MASK + window, t] = 1
    rows[R_MAX:R_MAX + 2] = 1
    w_tile = window.reshape(TILES, P).T
    q_mask = np.where(w_tile[:, :, None] == np.arange(4), 0, NEG).astype(np.float32)
    in_seg = np.stack([np.isin(w_tile, s) for s in ((1, 3), (1, 2, 3), (2, 3))], axis=1)
    p_mask = np.repeat(np.where(in_seg, 0, NEG)[:, :, :, None], HEADS, axis=3).reshape(P, NSEG, -1).astype(np.float32)
    h_mask = (np.arange(GF)[:, None] // HD == np.arange(GH)).astype(np.float32)
    const = {k: dram("c_" + k, a) for k, a in zip(CONSTS, (np.eye(P, dtype=np.float32), rows, q_mask, p_mask, h_mask))}

    out = nc.dram_tensor("out", (IMAGES, SIDE, SIDE, D), F32, kind="ExternalOutput").ap()
    build(nc, x, layers, const, out)
    r = run_bass_kernel_spmd(nc, [arrays], core_ids=[0])
    return r.results[0]["out"]
```
